# Optimizing a Trainium2 kernel written in Bass

```python
import numpy as np
import jax
import jax.numpy as jnp

def _softmax(x, axis=-1):
    return jax.nn.softmax(x, axis=axis)

def _gelu(x):
    return jax.nn.gelu(x, approximate=True)

def _silu(x):
    return jax.nn.silu(x)

def _sigmoid(x):
    return jax.nn.sigmoid(x)

def _layernorm(x, axis=-1, eps=1e-05):
    m = jnp.mean(x, axis=axis, keepdims=True)
    v = jnp.var(x, axis=axis, keepdims=True)
    return (x - m) / jnp.sqrt(v + eps)

def _scatter_add(tgt, idx, src, axis=0):
    return tgt.at[idx].add(src)

def _segment_sum(src, seg, n):
    return jax.ops.segment_sum(src, seg, n)
kernel_name = 'mk_gps_d1_gnn_r8_aeca87'

def setup_inputs(seed: int=0):
    np.random.seed(seed)
    _w = jnp.asarray

    def _rec_inputs():
        import jax
        import jax.numpy as jnp
        _gk = jax.random.key(seed)
        x = -0.0002117 + 1 * jax.random.normal(jax.random.fold_in(_gk, 1), (6250, 256), jnp.float32)
        _s = jax.random.randint(jax.random.fold_in(_gk, 2), (50000,), 0, 6250, jnp.int32)
        _d = jax.random.randint(jax.random.fold_in(_gk, 3), (50000,), 0, 6250, jnp.int32)
        _loop = jnp.arange(6250, dtype=jnp.int32)
        src = jnp.concatenate([_s, _d, _loop])
        dst = jnp.concatenate([_d, _s, _loop])
        _o = jnp.argsort(dst, stable=True)
        src = src[_o]
        dst = dst[_o]
        return (x, src, dst)
    x, src, dst = _rec_inputs()

    def _L0_gnn_setup():
        import jax, jax.numpy as jnp
        import numpy as np
        N_NODES = 12500
        N_EDGES = 400000
        D_IN = 256
        D_OUT = 256
        LEAKY_SLOPE = 0.01
        key = jax.random.key(seed)
        ks = jax.random.split(key, 8)
        s_in = 1.0 / np.sqrt(D_IN)
        s_out = 1.0 / np.sqrt(D_OUT)
        return {'features': jax.random.normal(ks[0], (N_NODES, D_IN), dtype=jnp.float32), 'indices': jax.random.randint(ks[1], (2, N_EDGES), 0, N_NODES, dtype=jnp.int64), 'W_layer': jax.random.uniform(ks[2], (D_OUT, D_IN), jnp.float32, -s_in, s_in), 'b_layer': jax.random.uniform(ks[3], (D_OUT,), jnp.float32, -s_in, s_in), 'w_a1': jax.random.uniform(ks[4], (1, D_OUT), jnp.float32, -s_out, s_out), 'b_a1': jax.random.uniform(ks[5], (1,), jnp.float32, -s_out, s_out), 'w_a2': jax.random.uniform(ks[6], (1, D_OUT), jnp.float32, -s_out, s_out), 'b_a2': jax.random.uniform(ks[7], (1,), jnp.float32, -s_out, s_out)}
    _L0_gnn_all = _L0_gnn_setup()
    _L0_gnn_in = {k: v for k, v in _L0_gnn_all.items() if k in ('W_layer', 'b_layer', 'w_a1', 'b_a1', 'w_a2', 'b_a2')}
    del _L0_gnn_all

    def _L0_mix_setup():
        import math
        import jax, jax.numpy as jnp
        import numpy as np
        EPS_DIV = 1e-07
        EPS_NORM = 1e-12

        def _l2_normalize(x, axis):
            n = jnp.sqrt(jnp.sum(x * x, axis=axis, keepdims=True))
            return x / jnp.maximum(n, EPS_NORM)
        key = jax.random.key(seed)
        ks = jax.random.split(key, 5)
        b, N, C = (8, 512, 256)
        x = jax.random.normal(ks[0], (b, N, C), dtype=jnp.float32)
        W_qkv = jax.random.normal(ks[1], (C, 3 * C), dtype=jnp.float32) * (1.0 / math.sqrt(C))
        b_qkv = jax.random.normal(ks[2], (3 * C,), dtype=jnp.float32) * 0.02
        W_out = jax.random.normal(ks[3], (C, C), dtype=jnp.float32) * (1.0 / math.sqrt(C))
        b_out = jax.random.normal(ks[4], (C,), dtype=jnp.float32) * 0.02
        return {'x': x, 'W_qkv': W_qkv, 'b_qkv': b_qkv, 'W_out': W_out, 'b_out': b_out}
    _L0_mix_all = _L0_mix_setup()
    _L0_mix_in = {k: v for k, v in _L0_mix_all.items() if k in ('W_qkv', 'b_qkv', 'W_out', 'b_out')}
    del _L0_mix_all

    def _L0_ffn_setup():
        import jax, jax.numpy as jnp
        import numpy as np
        N_EXPERTS = 8
        TOP_K = 2
        key = jax.random.key(seed)
        ks = jax.random.split(key, 5)
        B, T, C, E, H = (8, 256, 256, 8, 682)
        scale = 1.0 / np.sqrt(C)
        return {'x': jax.random.normal(ks[0], (B, T, C), dtype=jnp.float32), 'router_w': jax.random.normal(ks[1], (E, C), dtype=jnp.float32) * scale, 'w1': jax.random.normal(ks[2], (E, H, C), dtype=jnp.float32) * scale, 'w2': jax.random.normal(ks[3], (E, C, H), dtype=jnp.float32) * (1.0 / np.sqrt(H)), 'w3': jax.random.normal(ks[4], (E, H, C), dtype=jnp.float32) * scale}
    _L0_ffn_all = _L0_ffn_setup()
    _L0_ffn_in = {k: v for k, v in _L0_ffn_all.items() if k in ('router_w', 'w1', 'w2', 'w3')}
    del _L0_ffn_all
    return {'x': x, 'src': src, 'dst': dst, 'L0_gnn_W_layer': _L0_gnn_in['W_layer'], 'L0_gnn_b_layer': _L0_gnn_in['b_layer'], 'L0_gnn_w_a1': _L0_gnn_in['w_a1'], 'L0_gnn_b_a1': _L0_gnn_in['b_a1'], 'L0_gnn_w_a2': _L0_gnn_in['w_a2'], 'L0_gnn_b_a2': _L0_gnn_in['b_a2'], 'L0_mix_W_qkv': _L0_mix_in['W_qkv'], 'L0_mix_b_qkv': _L0_mix_in['b_qkv'], 'L0_mix_W_out': _L0_mix_in['W_out'], 'L0_mix_b_out': _L0_mix_in['b_out'], 'L0_ffn_router_w': _L0_ffn_in['router_w'], 'L0_ffn_w1': _L0_ffn_in['w1'], 'L0_ffn_w2': _L0_ffn_in['w2'], 'L0_ffn_w3': _L0_ffn_in['w3']}

def reference(x, src, dst, L0_gnn_W_layer, L0_gnn_b_layer, L0_gnn_w_a1, L0_gnn_b_a1, L0_gnn_w_a2, L0_gnn_b_a2, L0_mix_W_qkv, L0_mix_b_qkv, L0_mix_W_out, L0_mix_b_out, L0_ffn_router_w, L0_ffn_w1, L0_ffn_w2, L0_ffn_w3):
    import jax
    import jax.numpy as jnp

    def _L0_gnn_ref(features, indices, W_layer, b_layer, w_a1, b_a1, w_a2, b_a2):
        import jax, jax.numpy as jnp
        import numpy as np
        N_NODES = 12500
        N_EDGES = 400000
        D_IN = 256
        D_OUT = 256
        LEAKY_SLOPE = 0.01
        n = features.shape[0]
        h = features @ W_layer.T + b_layer
        a1 = (h @ w_a1.T + b_a1)[:, 0]
        a2 = (h @ w_a2.T + b_a2)[:, 0]
        row = indices[0]
        col = indices[1]
        v = jax.nn.leaky_relu(a1[row] + a2[col], negative_slope=LEAKY_SLOPE)
        m = jax.ops.segment_max(v, row, num_segments=n)
        ev = jnp.exp(v - m[row])
        s = jax.ops.segment_sum(ev, row, num_segments=n)
        att = ev / s[row]
        out = jax.ops.segment_sum(att[:, None] * h[col], row, num_segments=n)
        return out

    def _L0_mix_ref(x, W_qkv, b_qkv, W_out, b_out):
        import math
        import jax, jax.numpy as jnp
        import numpy as np
        EPS_DIV = 1e-07
        EPS_NORM = 1e-12

        def _l2_normalize(x, axis):
            n = jnp.sqrt(jnp.sum(x * x, axis=axis, keepdims=True))
            return x / jnp.maximum(n, EPS_NORM)
        b, N, C = x.shape
        qkv = x @ W_qkv + b_qkv
        q, k, v = jnp.split(qkv, 3, axis=2)
        q = q - jnp.mean(q, axis=2, keepdims=True)
        k = k - jnp.mean(k, axis=2, keepdims=True)
        q2 = q * q
        k2 = k * k
        q2s = jnp.sum(q2, axis=2, keepdims=True)
        k2s = jnp.sum(k2, axis=2, keepdims=True)
        k2 = _l2_normalize(k2 / (k2s + EPS_DIV), axis=-2)
        q2 = _l2_normalize(q2 / (q2s + EPS_DIV), axis=-1)
        kv = jnp.einsum('bnc,bnd->bcd', k2, v)
        t2 = jnp.einsum('bnc,bcd->bnd', q2, kv) / math.sqrt(N)
        attn = v + t2
        return attn @ W_out + b_out

    def _L0_ffn_ref(x, router_w, w1, w2, w3):
        import jax, jax.numpy as jnp
        import numpy as np
        N_EXPERTS = 8
        TOP_K = 2
        B, T, C = x.shape
        flat = x.reshape(-1, C)
        logits = flat @ router_w.T
        probs = jax.nn.softmax(logits, axis=-1)
        topk_probs, topk_idx = jax.lax.top_k(probs, TOP_K)
        topk_probs = topk_probs / (jnp.sum(topk_probs, axis=-1, keepdims=True) + 1e-09)
        onehot = jax.nn.one_hot(topk_idx, N_EXPERTS, dtype=flat.dtype)
        gates = jnp.einsum('nk,nke->ne', topk_probs, onehot)
        h1 = jnp.einsum('nc,ehc->neh', flat, w1)
        h3 = jnp.einsum('nc,ehc->neh', flat, w3)
        h = jax.nn.silu(h1) * h3
        y = jnp.einsum('neh,ech->nec', h, w2)
        out = jnp.einsum('ne,nec->nc', gates, y)
        return out.reshape(B, T, C)
    edge_index = jnp.stack([src, dst])
    xn = _layernorm(x, axis=-1)
    x = x + _L0_gnn_ref(xn, edge_index, L0_gnn_W_layer, L0_gnn_b_layer, L0_gnn_w_a1, L0_gnn_b_a1, L0_gnn_w_a2, L0_gnn_b_a2) + _L0_mix_ref(xn[None], L0_mix_W_qkv, L0_mix_b_qkv, L0_mix_W_out, L0_mix_b_out)[0]
    x = x + _L0_ffn_ref(_layernorm(x, axis=-1)[None], L0_ffn_router_w, L0_ffn_w1, L0_ffn_w2, L0_ffn_w3)[0]
    return x

_drawn_inputs = setup_inputs


def setup_inputs(seed=0):
    import zlib

    import numpy as np

    out = dict(_drawn_inputs(seed))
    spreads = {}
    factors = {'L0_gnn_w_a1': 2.788}
    for name, (base, spread) in spreads.items():
        noise = np.random.default_rng([zlib.crc32(name.encode()), seed]).standard_normal(out[name].shape)
        drawn = base * np.exp(spread * noise) if base else spread * noise
        out[name] = jnp.asarray(drawn.astype(out[name].dtype))
    for name, factor in factors.items():
        out[name] = (out[name] * factor).astype(out[name].dtype)
    return out
```

```python
from contextlib import ExitStack

import concourse.bass as bass
from concourse import mybir

ALU = mybir.AluOpType
ACT = mybir.ActivationFunctionType
AX = mybir.AxisListType
F32 = mybir.dt.float32
I32 = mybir.dt.int32
BF16 = mybir.dt.bfloat16

P = 128
N = 6250
C = 256
E = 106250
NT = 50
LAST = N - 48 * P
FULL = E // P
TAIL = E - FULL * P
EC = 16
ET = -(-(FULL + 1) // (2 * EC)) * 2 * EC
NCH = ET // EC
GT = 880
G = 4
NG = GT // G
RING = 8
TW = C + 2
DUMMY = NT * P
F = 682
FH = F // 2
FC = 6
FL = F - 5 * P
NE = 8
MT = 106
SHOW = []
SLOPE = 0.01
EPS = 1e-5


def build(nc, x, src, dst, w_h, w_hT, b_h, w_a, b_a, w_qkv, w_vT, b_qkv, w_out, b_out, b_cols, w_router, w13, w2, out):
    assert (E + 49 * 127) // P + -(-(ET * P - E) // P) <= GT and (2 * N + NE * 127) // P <= MT
    ctx = ExitStack()
    with ctx:
        def sem(name):
            return ctx.enter_context(nc.semaphore(name))

        def bank(name):
            return ctx.enter_context(nc.psum_tensor(name, [P, 512], F32))

        def dram(name, shape, dt):
            return nc.dram_tensor(name, shape, dt, **({"kind": "ExternalOutput"} if name in SHOW else {})).ap()

        rec_d = dram("edge_records", [P * GT, 2], I32)
        table_d = dram("table", [DUMMY + 1, TW], F32)
        q2t_d = dram("q2_transposed", [NT, P, 2 * P], F32)
        base_d = dram("base", [NT, P, C], F32)
        base2_d = dram("base2", [NT, P, C], F32)
        x2_d = dram("x2", [NT, P, C], F32)
        xn2_d = dram("xn2", [NT, P, C], F32)
        xs_d = dram("expert_in", [MT * P, C], F32)
        ys_d = dram("expert_out", [MT * P, C], F32)

        ACC_W, W2_W, W13_W = NT * TW, NE * FC * C, NE * 2 * 2 * F
        R1, R2, R3, R4 = 0, ACC_W, ACC_W + W2_W, ACC_W + W2_W + W13_W
        arena = ctx.enter_context(nc.sbuf_tensor("arena", [P, 52900], F32))
        at = {1: R1, 2: R2, 3: R3, 4: R4}
        ends = {1: R3, 2: R3, 3: R4, 4: 52900}

        def take(region, width, dt=F32, parts=P):
            a = at[region]
            at[region] += width
            assert at[region] <= ends[region], (region, dict(at))
            v = arena[0:parts, a:a + width]
            return v if dt == F32 else v.bitcast(dt)

        def restart(region):
            at[region] = {1: R1, 2: R2, 3: R3, 4: R4}[region]

        w13_sb = arena[:, R3:R4]
        ident, ones, before, iota = take(4, P), take(4, P), take(4, P), take(4, P)
        zeros = take(4, 512)
        iota_i = take(4, P, I32)
        a12 = take(4, 2 * NT)
        shift = take(4, 1)
        valid = take(4, NT)
        small = take(4, 64)
        gate = take(4, 2 * NT)
        pos_i = take(4, 2 * NT, I32)
        et_i = take(4, P, I32)
        router = take(4, 2 * NE)
        row_i, col_i, hi_i = take(1, ET, I32), take(1, ET, I32), take(1, ET, I32)
        ohb, prod = arena[:, R1:R1 + GT], arena[:, R1 + GT:R1 + 2 * GT]
        rec = take(1, 2 * ET, I32)
        hi_f = take(1, ET)
        mask = take(1, ET // 2, BF16)
        slot_i = take(1, ET, I32)
        onehot = take(1, EC * NT)
        chunk_pos = take(1, EC)
        chunk_i = take(1, 2 * EC, I32)
        run = take(1, 2 * NT)
        junk = take(1, NT)
        idx_ring = take(1, 2 * EC, I32)
        rec_ring = take(1, 4 * EC, I32)
        hist = take(1, NT)
        scan = take(1, 2 * (64 + NT))
        tiles_i = take(1, NT, I32)
        first = take(1, 2 * NT)
        edge = take(1, 2)
        bweight = take(1, 1)
        at[2] = at[1]
        rec_init = take(2, 2 * GT, I32)
        wcat = take(2, 2 * (4 * C + 2))
        wnat = take(2, 2 * C)
        wa_sb = take(2, 4)
        wvt_sb, wout_sb = take(2, 2 * C), take(2, 2 * C)
        bias = take(2, 4 * C + 2)
        at_p = at[2]

        psum = [bank(f"bank{i}") for i in range(8)]
        s = {}

        carry = {}
        for j in range(4):
            n = len(range(j, N // P + 1, 4))
            carry[f"x2_in{j}"] = (f"xd_in{j}", 16 * n)
            carry[f"y_in{j}"] = (f"sent{j}", 32 * n)
        for b in range(2):
            carry[f"mix_in{b}"] = (f"x_in{b}", 8 * NT)
            carry[f"b2_in{b}"] = (f"x_in{b}", 24 * NT)
            carry[f"xs_in{b}"] = (f"x_in{b}", 32 * NT)
            carry[f"mix_out{b}"] = (f"row_out{b}", 24 * NT)
            carry[f"xn2_out{b}"] = (f"row_out{b}", 32 * NT)
            carry[f"yo_out{b}"] = (f"row_out{b}", 40 * NT)
        for new, old_, count in (("gg_turned", "xn2_turned", NT), ("logits_done", "q2t_done", NT), ("xn2t_ready", "xnt_ready", NT),
                                 ("y_done", "hv_done", NT), ("yo_ready", "q2_ready", NT), ("x2_ready", "xn_ready", NT),
                                 ("xst_ready", "kn2_ready", NT), ("logits_ready", "kn_ready", NT), ("xn2_ready", "qk_taken", NT),
                                 ("gg0_ready", "hv_taken", NT), ("gg1_ready", "base_ready", NT), ("mv_ready", "table_ready", NT),
                                 ("sig0_ready", "k2_ready", NT), ("sig1_ready", "q4_ready", NT), ("hidden0_done", "sums_done", NT),
                                 ("hidden1_done", "xnt_done", NT), ("sum_ready", "mix_ready", NT), ("xs_turned", "mix_done", NT)):
            carry[new] = (old_, count)

        def S(name):
            name = carry.get(name, (name, 0))[0]
            if name not in s:
                s[name] = sem(name)
            return s[name]

        def after(name, value):
            return value + carry[name][1]

        def due(value):
            return not isinstance(value, int) or value > 0

        class Order:

            def __init__(self, eng, name):
                self.eng, self.name, self.n = eng, name, 0

            def __call__(self, ins):
                self.n += 1
                ins.then_inc(S(self.name), 1)
                return ins

        def phase(eng, k):
            eng.drain().then_inc(S("stage_done"), 1)
            eng.wait_ge(S("stage_done"), 5 * k)

        QK, H0, VO0, A0 = 0, 2 * C, 3 * C, 4 * C
        wc = wcat.rearrange("p (k n) -> p k n", k=2)
        x_in = [take(2, C) for _ in range(2)]
        xn = [take(2, C) for _ in range(2)]
        xnt = [take(2, C) for _ in range(2)]
        qk = take(2, 2 * C)
        q2, q4, k2, kn, kn2 = (take(2, C) for _ in range(5))
        gt_sb = take(2, 2 * C)
        g1_row, bvo_row = take(2, C, parts=1), take(2, C, parts=1)
        hb = [take(2, TW) for _ in range(2)]
        base = [take(2, C) for _ in range(2)]
        q2t = [take(2, C) for _ in range(2)]
        mix_q = [take(2, C) for _ in range(2)]
        mix_b = [take(2, C) for _ in range(2)]
        mix_o = [take(2, C) for _ in range(2)]
        b_col = take(2, 4)
        bo_row = take(2, C)
        mean_w = take(2, 8)
        lane_i = take(2, NT, I32)
        q2s, q4s, fac, fac2 = (take(2, NT) for _ in range(4))
        st6, mv, rstd = take(2, 12), take(2, 2), take(2, 2)
        k2s, rk, rkv = take(2, 1), take(2, 1), take(2, 1)
        kscale = take(2, 2)
        kw_sb = take(4, 2 * C)

        a1_rows = take(2, P)
        a1t_at = at[4]
        a1t, same = take(4, GT), take(4, GT)
        bt_i = take(4, GT, I32)
        tile_f, tile_i = same, bt_i
        restart(2)
        acc = arena[:, R1:R1 + ACC_W]
        rec_all = take(2, 2 * GT, I32)
        lane_row = take(2, GT)
        late = [arena[:, R4 - 4 * F + n * G * TW:R4 - 4 * F + (n + 1) * G * TW] for n in range(2)]
        rows_in = [take(2, G * TW) for _ in range(RING - 2)] + late
        masked = [take(2, G * P) for _ in range(3)] + [arena[:, R4 - G * P:R4]]
        member = [take(2, G * P) for _ in range(2)]
        weight = [take(2, G * P), kw_sb]
        idx_g = [take(2, G, I32) for _ in range(RING)]
        a2s = [take(2, G) for _ in range(2)]
        tile_max = take(2, G)
        nb = [take(2, G) for _ in range(2)]
        lin = take(2, G)
        lb = [take(2, 2 * G + 1) for _ in range(2)]
        dm0, dm = take(2, G), take(2, G)
        alpha = [take(2, G) for _ in range(RING)]
        score, leaky, zarg = take(2, G), take(2, G), take(2, G)
        rec_a2 = [take(2, G) for _ in range(4)]
        wexp = [take(2, G) for _ in range(2)]
        wscale = [take(2, G) for _ in range(2)]
        at[4] = a1t_at
        b2 = [take(4, C) for _ in range(2)]
        xn2 = [take(4, C) for _ in range(2)]
        xn2t = [take(4, C) for _ in range(2)]
        logits = take(4, NT * NE)
        rden, rstd2 = take(4, NT), take(4, NT)
        mv2 = take(4, 2 * NT)
        st2, mvt = take(4, 6), take(4, 2)
        restart(1)
        nidx = take(1, NE)
        oh12 = take(1, 2 * NT * NE)
        scr = take(1, 2 * NT * NE)
        pre_a, pre_b = take(1, 2 * NT * NE), take(1, 2 * NT * NE)
        top = take(1, 2 * NT)
        ti = take(1, NT)
        pz = take(1, 4 * NT)
        escan = take(1, 2 * (NE + NE))
        etile_i = take(1, NE, I32)
        efirst, eend, ebase = take(1, NE), take(1, NE), take(1, NE)
        tot = take(1, NE)
        tcmp = take(1, P * NE)
        ecount = take(1, P)
        pos_f = take(1, 2 * NT)
        xd = [take(1, C) for _ in range(4)]
        idx_d = [take(1, 2, I32) for _ in range(4)]
        y1 = [take(1, C) for _ in range(4)]
        y2 = [take(1, C) for _ in range(4)]
        restart(1)
        xs = [take(1, C) for _ in range(2)]
        xst = [take(1, C) for _ in range(2)]
        sig = [take(1, FH) for _ in range(2)]
        prod1 = [take(1, FH) for _ in range(2)]
        gg = [take(1, F) for _ in range(2)]
        ggt = [take(1, FC * P) for _ in range(2)]
        yo = [take(1, C) for _ in range(2)]
        w2_sb = arena[:, R2:R3]

        def ds(i, n=1):
            return slice(i, i + n) if isinstance(i, int) else bass.ds(i, n)

        def tile_of(t, j):
            return t[j] if isinstance(j, int) else t[bass.ds(j, 1), :, :].rearrange("a p c -> (a p) c")

        block = ctx.enter_context(nc.Block())
        from_here = dict(at)

        row_src = src[0:FULL * P].rearrange("(p t) -> p t", p=P)
        col_src = dst[0:FULL * P].rearrange("(p t) -> p t", p=P)

        def sort_sync(sp):
            sp.wait_ge(S("edges_cleared"), 1)
            sp.dma_start(row_i[:, 0:FULL], row_src).then_inc(S("edges_in"), 16)
            sp.dma_start(col_i[:, 0:FULL], col_src).then_inc(S("edges_in"), 16)
            sp.dma_start(row_i[0:TAIL, FULL:FULL + 1], src[FULL * P:E].rearrange("(p o) -> p o", o=1)).then_inc(S("edges_in"), 16)
            sp.dma_start(col_i[0:TAIL, FULL:FULL + 1], dst[FULL * P:E].rearrange("(p o) -> p o", o=1)).then_inc(S("edges_in"), 16)
            for e in range(NE - 1):
                sp.dma_start(w13_sb[:, e * 4 * F:(e + 1) * 4 * F], w13[:, e * 4 * F:(e + 1) * 4 * F]).then_inc(S("w13_in"), 16)
            sp.wait_ge(S("rec_init_ready"), 2)
            sp.dma_start(rec_d.rearrange("(p t) c -> p (t c)", p=P), rec_init[:, :]).then_inc(S("rec_cleared"), 16)
        def project_sync(sp):
            def ld(dst_, src_):
                sp.dma_start(dst_, src_).then_inc(S("weights_in"), 16)
            rows = "(k p) n -> p k n"
            ld(wc[:, :, QK:QK + 2 * C], w_qkv[:, 0:2 * C].rearrange(rows, p=P))
            ld(wc[:, :, H0:H0 + C], w_hT.rearrange(rows, p=P))
            ld(wnat.rearrange("p (k n) -> p k n", k=2), w_h.rearrange(rows, p=P))
            ld(wa_sb.rearrange("p (k n) -> p k n", k=2), w_a.rearrange(rows, p=P))
            ld(wvt_sb.rearrange("p (k n) -> p k n", k=2), w_vT.rearrange(rows, p=P))
            ld(wout_sb.rearrange("p (k n) -> p k n", k=2), w_out.rearrange(rows, p=P))
            ld(bias[:, QK:QK + 2 * C], b_qkv[0:2 * C].unsqueeze(0).to_broadcast([P, 2 * C]))
            ld(bias[:, H0:H0 + C], b_h.unsqueeze(0).to_broadcast([P, C]))
            ld(bias[:, A0:A0 + 2], b_a.unsqueeze(0).to_broadcast([P, 2]))
            ld(bo_row[:, :], b_out.unsqueeze(0).to_broadcast([P, C]))
            ld(b_col[:, :], b_cols)

            def step(i, b):
                if not (isinstance(i, int) and i >= NT):
                    if due(i - 1):
                        sp.wait_ge(S("base_ready"), i - 1)
                    sp.dma_start(x_in[b][:, :], x.rearrange("(t p) c -> t p c", p=P)[i] if isinstance(i, int)
                                 else x.rearrange("(t p) c -> t p c", p=P)[bass.ds(i, 1), :, :].rearrange("a p c -> (a p) c"))\
                        .then_inc(S(f"x_in{b}"), 16)
                if not (isinstance(i, int) and i < 2):
                    j = i - 2
                    def tile_of(t):
                        return t[j] if isinstance(j, int) else t[bass.ds(j, 1), :, :].rearrange("a p c -> (a p) c")
                    if due(j + 1):
                        sp.wait_ge(S("table_ready"), j + 1)
                    sp.dma_start(tile_of(table_d[0:NT * P, :].rearrange("(t p) c -> t p c", p=P)), hb[b][:, :]).then_inc(S(f"row_out{b}"), 16)
                    if due(j + 1):
                        sp.wait_ge(S("base_ready"), j + 1)
                    sp.dma_start(tile_of(base_d), base[b][:, :]).then_inc(S(f"row_out{b}"), 16)
                    if due(j + 1):
                        sp.wait_ge(S("q2t_ready"), j + 1)
                    sp.dma_start(tile_of(q2t_d), q2t[b][:, :]).then_inc(S(f"row_out{b}"), 16)

            step(0, 0)
            step(1, 1)
            with sp.Fori(1, NT // 2) as k:
                step(k * 2, 0)
                step(k * 2 + 1, 1)
            step(NT, 0)
            step(NT + 1, 1)
            sp.wait_ge(S("zeros_ready"), 1)
            sp.dma_start(table_d[DUMMY:DUMMY + 1, :], zeros[0:1, 0:TW]).then_inc(S("cleared"), 16)
            sp.dma_start(xs_d.rearrange("(p a r) c -> p a (r c)", p=P, r=2),
                         zeros.unsqueeze(1).to_broadcast([P, MT // 2, 512])).then_inc(S("cleared"), 16)
            sp.wait_ge(S("row_out0"), 48 * (NT // 2))
            sp.wait_ge(S("row_out1"), 48 * (NT // 2))
            sp.wait_ge(S("cleared"), 32)

        def project_tensor(pe):
            mm = nc.tensor.matmul
            pe.wait_ge(S("weights_in"), 16 * 11)
            wo = wout_sb.rearrange("p (k n) -> p k n", k=2)
            for c in range(2):
                for j in range(2):
                    mm(psum[1][:, c * C:(c + 1) * C], wvt_sb[:, j * C + c * P:j * C + c * P + P], wo[:, j, :],
                       start=(j == 0), stop=(j == 1))
            for c in range(2):
                for j in range(2):
                    mm(psum[2][:, 2 * c:2 * c + 2], wnat[:, j * C + c * P:j * C + c * P + P], wa_sb[:, 2 * j:2 * j + 2],
                       start=(j == 0), stop=(j == 1))
            for j in range(2):
                mm(psum[3][:, 0:C], b_col[:, j:j + 1].to_broadcast([P, P]), wo[:, j, :], start=(j == 0), stop=(j == 1))
            for j in range(2):
                last = mm(psum[4][:, 0:2], b_col[:, 2 + j:3 + j].to_broadcast([P, P]), wa_sb[:, 2 * j:2 * j + 2],
                          start=(j == 0), stop=(j == 1))
            last.then_inc(S("folded"), 1)
            pe.wait_ge(S("zeros_ready"), 1)
            mm(psum[5][:, :], ident[:, :], zeros[:, :], start=True, stop=False, skip_group_check=True)
            mm(psum[6][:, :], ident[:, :], zeros[:, :], start=True, stop=False, skip_group_check=True)
            pe.wait_ge(S("wcat_ready"), 1)

            def step(i, b):
                if not (isinstance(i, int) and i >= NT):
                    pe.wait_ge(S("xn_ready"), i + 1)
                    if due(i):
                        pe.wait_ge(S("xnt_ready"), i)
                    nc.tensor.transpose(psum[3][:, 0:P], xn[b][:, 0:P], ident[:, :])
                    nc.tensor.transpose(psum[3][:, P:C], xn[b][:, P:C], ident[:, :]).then_inc(S("xnt_done"), 1)
                    pe.wait_ge(S("xnt_ready"), i + 1)
                    if due(i - 1):
                        pe.wait_ge(S("qk_taken"), i - 1)
                    for c in range(2):
                        mm(psum[b][:, :], xnt[b][:, c * P:(c + 1) * P], wc[:, c, QK:QK + 2 * C], start=(c == 0), stop=(c == 1))\
                            .then_inc(S("qk_half"), 1)
                    if due(i):
                        pe.wait_ge(S("hv_taken"), i)
                    for c in range(2):
                        mm(psum[2][:, :], xnt[b][:, c * P:(c + 1) * P], wc[:, c, H0:H0 + 2 * C], start=(c == 0), stop=(c == 1))
                    for c in range(2):
                        last = mm(psum[7][:, 0:2], xnt[b][:, c * P:(c + 1) * P], wc[:, c, A0:A0 + 2], start=(c == 0), stop=(c == 1))
                    last.then_inc(S("hv_done"), 1)
                if not (isinstance(i, int) and i < 1):
                    j = i - 1
                    if due(j + 1):
                        pe.wait_ge(S("q2_ready"), j + 1)
                    if due(j):
                        pe.wait_ge(S("q2t_ready"), j)
                    nc.tensor.transpose(psum[4][:, 0:P], q2[:, 0:P], ident[:, :])
                    nc.tensor.transpose(psum[4][:, P:C], q2[:, P:C], ident[:, :]).then_inc(S("q2t_done"), 1)
                    if due(j + 1):
                        pe.wait_ge(S("kn_ready"), j + 1)
                    for c in range(2):
                        mm(psum[5][:, c * C:(c + 1) * C], xn[1 - b][:, c * P:(c + 1) * P], kn[:, :], start=False, stop=False,
                           skip_group_check=True)
                    mm(psum[6][0:1, 0:C], ones[:, 0:1], kn[:, :], start=False, stop=False, skip_group_check=True)
                    if due(j + 1):
                        pe.wait_ge(S("kn2_ready"), j + 1)
                    for c in range(2):
                        last = mm(psum[6][:, C + c:C + c + 1], kn2[:, c * P:(c + 1) * P], ones[:, 0:1], start=False, stop=False,
                                  skip_group_check=True)
                    last.then_inc(S("sums_done"), 1)

            step(0, 0)
            step(1, 1)
            with pe.Fori(1, NT // 2) as k:
                step(k * 2, 0)
                step(k * 2 + 1, 1)
            step(NT, 0)

        def project_scalar(act):
            a = nc.scalar.activation

            def step(i, b):
                if not (isinstance(i, int) and i >= NT):
                    act.wait_ge(S("var_ready"), i + 1)
                    a(rstd[:, 1:2], rstd[:, 0:1], ACT.Sqrt).then_inc(S("std_ready"), 1)
                    act.wait_ge(S("xnt_done"), i + 1)
                    a(xnt[b][:, :], psum[3][:, 0:C], ACT.Copy).then_inc(S("xnt_ready"), 1)
                if not (isinstance(i, int) and i < 1):
                    j = i - 1
                    if due(j + 1):
                        act.wait_ge(S("qk_taken"), j + 1)
                    if due(j):
                        act.wait_ge(S("kn_ready"), j)
                    a(k2[:, :], qk[:, C:2 * C], ACT.Square, accum_out=k2s[:, :]).then_inc(S("k2_ready"), 1)
                    if due(j):
                        act.wait_ge(S("q2t_done"), j)
                    if due(j):
                        act.wait_ge(S("q4_ready"), j)
                    col = slice(j, j + 1) if isinstance(j, int) else bass.ds(j, 1)
                    a(q2[:, :], qk[:, 0:C], ACT.Square, accum_out=q2s[:, col]).then_inc(S("q2_ready"), 1)
                    if due(j + 1):
                        act.wait_ge(S("q2_ready"), j + 1)
                    a(q4[:, :], q2[:, :], ACT.Square, accum_out=q4s[:, col]).then_inc(S("q4_ready"), 1)
                    if due(j + 1):
                        act.wait_ge(S("q2t_done"), j + 1)
                    if not (isinstance(j, int) and j < 2):
                        if due((j - (1 - b)) * 24):
                            act.wait_ge(S(f"row_out{1 - b}"), (j - (1 - b)) * 24)
                    a(q2t[1 - b][:, :], psum[4][:, 0:C], ACT.Copy).then_inc(S("q2t_ready"), 1)
                    if due(j + 1):
                        act.wait_ge(S("kn_ready"), j + 1)
                    if due(j):
                        act.wait_ge(S("sums_done"), j)
                    a(kn2[:, :], kn[:, :], ACT.Square).then_inc(S("kn2_ready"), 1)

            step(0, 0)
            step(1, 1)
            with act.Fori(1, NT // 2) as k:
                step(k * 2, 0)
                step(k * 2 + 1, 1)
            step(NT, 0)

        def project_vector(dve):
            v = nc.vector
            o = Order(dve, "v_fold")
            dve.wait_ge(S("folded"), 1)
            dve.wait_ge(S("pool_lanes"), 1)
            o(v.tensor_scalar(valid[:, :], lane_i[:, :], float(N), None, ALU.is_lt))
            for c in range(2):
                v.tensor_copy(wc[:, c, VO0:VO0 + C], psum[1][:, c * C:(c + 1) * C])
                v.tensor_copy(wc[:, c, A0:A0 + 2], psum[2][:, 2 * c:2 * c + 2])
            v.tensor_copy(bvo_row[:, :], psum[3][0:1, 0:C])
            v.tensor_tensor(bias[:, VO0:VO0 + C], psum[3][:, 0:C], bo_row[:, :], ALU.add)
            o(v.tensor_tensor(bias[:, A0:A0 + 2], psum[4][:, 0:2], bias[:, A0:A0 + 2], ALU.add))
            for c in range(2):
                v.tensor_reduce(mean_w[:, 2 * c:2 * c + 2], wc[:, c, 0:2 * C].rearrange("p (m n) -> p m n", m=2), AX.X, ALU.add)
            o(v.tensor_reduce(mean_w[:, 4:6], bias[:, 0:2 * C].rearrange("p (m n) -> p m n", m=2), AX.X, ALU.add))
            dve.wait_ge(S("v_fold"), o.n)
            o(v.tensor_scalar(mean_w[:, 0:6], mean_w[:, 0:6], 1.0 / C, None, ALU.mult))
            dve.wait_ge(S("v_fold"), o.n)
            for c in range(2):
                for m in range(2):
                    v.tensor_scalar(wc[:, c, m * C:(m + 1) * C], wc[:, c, m * C:(m + 1) * C],
                                    mean_w[:, 2 * c + m:2 * c + m + 1], None, ALU.subtract)
            for m in range(2):
                last = v.tensor_scalar(bias[:, m * C:(m + 1) * C], bias[:, m * C:(m + 1) * C], mean_w[:, 4 + m:5 + m], None,
                                       ALU.subtract)
            for b in range(2):
                last = v.memset(hb[b][:, C:C + 1], 1.0)
            last.then_inc(S("wcat_ready"), 1)
            dve.wait_ge(S("wcat_ready"), 1)

            def step(i, b):
                if not (isinstance(i, int) and i >= NT):
                    dve.wait_ge(S(f"x_in{b}"), (i - b) * 8 + 16)
                    v.bn_stats(st6[:, 0:6], x_in[b][:, :]).then_inc(S("ln_steps"), 1)
                    dve.wait_ge(S("ln_steps"), i * 3 + 1)
                    dve.sem_inc(S("vector_steps"), 1)
                    v.bn_aggr(mv[:, :], st6[:, 0:6]).then_inc(S("ln_steps"), 1)
                    dve.wait_ge(S("ln_steps"), i * 3 + 2)
                    v.tensor_scalar(rstd[:, 0:1], mv[:, 1:2], EPS, None, ALU.add).then_inc(S("var_ready"), 1)
                    dve.wait_ge(S("std_ready"), i + 1)
                    v.reciprocal(rstd[:, 0:1], rstd[:, 1:2]).then_inc(S("ln_steps"), 1)
                    dve.wait_ge(S("ln_steps"), i * 3 + 3)
                    if due(i - 1):
                        dve.wait_ge(S("sums_done"), i - 1)
                    v.tensor_scalar(xn[b][:, :], x_in[b][:, :], mv[:, 0:1], rstd[:, 0:1], ALU.subtract, ALU.mult)\
                        .then_inc(S("xn_ready"), 1)
                if not (isinstance(i, int) and i < 1):
                    j, bj = i - 1, 1 - b
                    if due(j * 2 + 2):
                        dve.wait_ge(S("qk_half"), j * 2 + 2)
                    if due(j):
                        dve.wait_ge(S("q2_ready"), j)
                    v.tensor_tensor(qk[:, :], psum[bj][:, :], bias[:, 0:2 * C], ALU.add).then_inc(S("qk_taken"), 1)
                    if due(j + 1):
                        dve.wait_ge(S("hv_done"), j + 1)
                    if not (isinstance(j, int) and j < 2):
                        if due((j - bj) * 24):
                            dve.wait_ge(S(f"row_out{bj}"), (j - bj) * 24)
                    v.tensor_tensor(hb[bj][:, 0:C], psum[2][:, 0:C], bias[:, H0:H0 + C], ALU.add)
                    v.tensor_tensor(hb[bj][:, C + 1:C + 2], psum[7][:, 1:2], bias[:, A0 + 1:A0 + 2], ALU.add)
                    cols = slice(2 * j, 2 * j + 2) if isinstance(j, int) else bass.ds(j * 2, 2)
                    v.tensor_tensor(a12[:, cols], psum[7][:, 0:2], bias[:, A0:A0 + 2], ALU.add).then_inc(S("table_ready"), 1)
                    v.tensor_tensor(base[bj][:, :], psum[2][:, C:2 * C], bias[:, VO0:VO0 + C], ALU.add).then_inc(S("hv_taken"), 1)
                    if due(j + 1):
                        dve.wait_ge(S("hv_taken"), j + 1)
                    v.tensor_tensor(base[bj][:, :], base[bj][:, :], x_in[bj][:, :], ALU.add).then_inc(S("base_ready"), 1)
                    if due(j + 1):
                        dve.wait_ge(S("k2_ready"), j + 1)
                    v.tensor_scalar(rk[:, :], k2s[:, :], 1e-7, None, ALU.add).then_inc(S("k_steps"), 1)
                    dve.wait_ge(S("k_steps"), j * 3 + 1)
                    v.reciprocal(rk[:, :], rk[:, :]).then_inc(S("k_steps"), 1)
                    dve.wait_ge(S("k_steps"), j * 3 + 2)
                    col = slice(j, j + 1) if isinstance(j, int) else bass.ds(j, 1)
                    v.tensor_tensor(rkv[:, :], rk[:, :], valid[:, col], ALU.mult).then_inc(S("k_steps"), 1)
                    dve.wait_ge(S("k_steps"), j * 3 + 3)
                    if due(j):
                        dve.wait_ge(S("sums_done"), j)
                    if due(j):
                        dve.wait_ge(S("kn2_ready"), j)
                    v.tensor_scalar(kn[:, :], k2[:, :], rkv[:, :], None, ALU.mult).then_inc(S("kn_ready"), 1)

            step(0, 0)
            step(1, 1)
            with dve.Fori(1, NT // 2) as k:
                step(k * 2, 0)
                step(k * 2 + 1, 1)
            step(NT, 0)

        def mix_scalar(act):
            act.wait_ge(S("gt_copied"), 1)
            nc.scalar.activation(kscale[:, :], psum[6][:, C:C + 2], ACT.Sqrt)
            act.wait_ge(S("q4_ready"), NT)
            nc.scalar.activation(fac2[:, :], q4s[:, :], ACT.Sqrt).then_inc(S("roots_ready"), 1)

        def mix_sync(sp):
            def tile_of(t, j):
                return t[j] if isinstance(j, int) else t[bass.ds(j, 1), :, :].rearrange("a p c -> (a p) c")

            def step(i, b):
                if not (isinstance(i, int) and i >= NT):
                    if due(i - 1):
                        sp.wait_ge(S("mix_done"), i - 1)
                    if due(i - 1):
                        sp.wait_ge(S("mix_ready"), i - 1)
                    sp.dma_start(mix_q[b][:, :], tile_of(q2t_d, i)).then_inc(S(f"mix_in{b}"), 16)
                    sp.dma_start(mix_b[b][:, :], tile_of(base_d, i)).then_inc(S(f"mix_in{b}"), 16)
                if not (isinstance(i, int) and i < 1):
                    if due(i):
                        sp.wait_ge(S("mix_ready"), i)
                    sp.dma_start(tile_of(base2_d, i - 1), mix_o[1 - b][:, :]).then_inc(S(f"mix_out{1 - b}"), 16)

            step(0, 0)
            step(1, 1)
            with sp.Fori(1, NT // 2) as k:
                step(k * 2, 0)
                step(k * 2 + 1, 1)
            step(NT, 0)
            sp.wait_ge(S("mix_out0"), after("mix_out0", 16 * (NT // 2)))
            sp.wait_ge(S("mix_out1"), after("mix_out1", 16 * (NT // 2)))

        def mix_tensor(pe):
            mm = nc.tensor.matmul
            pe.wait_ge(S("gt_copied"), 1)
            for ck in range(2):
                for cx in range(2):
                    mm(psum[1][:, ck * C:(ck + 1) * C], gt_sb[:, cx * C + ck * P:cx * C + ck * P + P], wc[:, cx, VO0:VO0 + C],
                       start=(cx == 0), stop=False)
                last = mm(psum[1][:, ck * C:(ck + 1) * C], g1_row[:, ck * P:(ck + 1) * P], bvo_row[:, :], start=False, stop=True)
            last.then_inc(S("kw_done"), 1)
            pe.wait_ge(S("kw_ready"), 1)

            def step(i, b):
                pe.wait_ge(S(f"mix_in{b}"), after(f"mix_in{b}", (i - b) * 16 + 32))
                if due(i - 1):
                    pe.wait_ge(S("mix_ready"), i - 1)
                for c in range(2):
                    last = mm(psum[2 + b][:, 0:C], mix_q[b][:, c * P:(c + 1) * P], kw_sb[:, c * C:(c + 1) * C],
                              start=(c == 0), stop=(c == 1))
                last.then_inc(S("mix_done"), 1)

            step(0, 0)
            step(1, 1)
            with pe.Fori(1, NT // 2) as k:
                step(k * 2, 0)
                step(k * 2 + 1, 1)

        def mix_vector(dve):
            v = nc.vector
            o = Order(dve, "v_mix")
            dve.wait_ge(S("sums_done"), NT)
            v.tensor_copy(gt_sb[:, :], psum[5][:, :])
            v.tensor_copy(g1_row[:, :], psum[6][0:1, 0:C]).then_inc(S("gt_copied"), 1)
            dve.wait_ge(S("roots_ready"), 1)
            o(v.tensor_scalar(kscale[:, :], kscale[:, :], 1e-12, None, ALU.max))
            dve.wait_ge(S("v_mix"), o.n)
            o(v.reciprocal(kscale[:, :], kscale[:, :]))
            dve.wait_ge(S("q4_ready"), NT)
            o(v.tensor_scalar(fac[:, :], q2s[:, :], 1e-7, None, ALU.add))
            dve.wait_ge(S("v_mix"), o.n)
            o(v.reciprocal(fac[:, :], fac[:, :]))
            dve.wait_ge(S("v_mix"), o.n)
            o(v.tensor_tensor(fac2[:, :], fac2[:, :], fac[:, :], ALU.mult))
            dve.wait_ge(S("v_mix"), o.n)
            o(v.tensor_scalar(fac2[:, :], fac2[:, :], 1e-12, None, ALU.max))
            dve.wait_ge(S("v_mix"), o.n)
            o(v.reciprocal(fac2[:, :], fac2[:, :]))
            dve.wait_ge(S("v_mix"), o.n)
            o(v.tensor_tensor(fac[:, :], fac[:, :], fac2[:, :], ALU.mult))
            dve.wait_ge(S("kw_done"), 1)
            for ck in range(2):
                last = v.tensor_scalar(kw_sb[:, ck * C:(ck + 1) * C], psum[1][:, ck * C:(ck + 1) * C], kscale[:, ck:ck + 1],
                                       float(N) ** -0.5, ALU.mult, ALU.mult)
            last.then_inc(S("kw_ready"), 1)
            dve.wait_ge(S("v_mix"), o.n)

            def step(i, b):
                dve.wait_ge(S("mix_done"), i + 1)
                dve.wait_ge(S(f"mix_in{b}"), after(f"mix_in{b}", (i - b) * 16 + 32))
                if not (isinstance(i, int) and i < 2):
                    if due((i - b) * 8):
                        dve.wait_ge(S(f"mix_out{b}"), after(f"mix_out{b}", (i - b) * 8))
                col = slice(i, i + 1) if isinstance(i, int) else bass.ds(i, 1)
                v.scalar_tensor_tensor(mix_o[b][:, :], psum[2 + b][:, 0:C], fac[:, col], mix_b[b][:, :], ALU.mult, ALU.add)\
                    .then_inc(S("mix_ready"), 1)

            step(0, 0)
            step(1, 1)
            with dve.Fori(1, NT // 2) as k:
                step(k * 2, 0)
                step(k * 2 + 1, 1)

        def tables_tensor(pe):
            mm = nc.tensor.matmul
            H = GT // 2
            pe.wait_ge(S("mix_ready"), NT)
            nc.tensor.transpose(psum[0][0:NT, 0:P], first[:, 0:NT], ident[:, :])
            nc.tensor.transpose(psum[0][0:NT, P:2 * P], first[:, NT:2 * NT], ident[:, :])
            nc.tensor.transpose(psum[0][0:NT, 2 * P:3 * P], a12.rearrange("p (t c) -> p t c", c=2)[:, :, 0], ident[:, :])\
                .then_inc(S("turned"), 1)
            pe.wait_ge(S("a2_least"), 1)
            nc.tensor.transpose(psum[7][0:1, 0:P], small[:, 0:1], ident[:, :]).then_inc(S("least_turned"), 1)
            pe.wait_ge(S("tables_ready"), 1)
            for h in range(2):
                mm(psum[1 + h][:, 0:H], ones[0:NT, :], prod[0:NT, h * H:(h + 1) * H], start=True, stop=True)
                mm(psum[3 + h][:, 0:H], a1_rows[0:NT, :], ohb[0:NT, h * H:(h + 1) * H], start=True, stop=True)
                mm(psum[5 + h][0:1, 0:H], bweight[0:NT, :], ohb[0:NT, h * H:(h + 1) * H], start=True, stop=True)
            mm(psum[0][:, 0:1], ones[0:1, :], small[0:1, 2:3], start=True, stop=True).then_inc(S("tables_done"), 1)

        def tables_vector(dve):
            v = nc.vector
            o = Order(dve, "v_tables")
            H = GT // 2
            o(v.tensor_copy(tile_f[:, :], tile_i[:, :]))
            o(v.tensor_scalar(bweight[:, :], lane_i[:, 0:1], -1.0, float(NT - 1), ALU.mult, ALU.add))
            v.tensor_reduce(small[:, 0:1], a12.rearrange("p (t c) -> p t c", c=2)[:, :, 1], AX.X, ALU.min)\
                .then_inc(S("a2_least"), 1)
            dve.wait_ge(S("turned"), 1)
            v.tensor_copy(edge[0:NT, 0:1], psum[0][0:NT, 0:1])
            v.tensor_copy(edge[0:NT, 1:2], psum[0][0:NT, P:P + 1])
            o(v.tensor_copy(a1_rows[0:NT, :], psum[0][0:NT, 2 * P:3 * P]))
            dve.wait_ge(S("v_tables"), o.n)
            o(v.tensor_scalar(prod[0:NT, :], tile_f[0:NT, :], edge[0:NT, 1:2], None, ALU.is_lt))
            dve.wait_ge(S("v_tables"), o.n)
            o(v.scalar_tensor_tensor(ohb[0:NT, :], tile_f[0:NT, :], edge[0:NT, 0:1], prod[0:NT, :], ALU.is_ge, ALU.mult))
            dve.wait_ge(S("least_turned"), 1)
            o(v.tensor_reduce(small[0:1, 1:2], psum[7][0:1, 0:P], AX.X, ALU.min))
            dve.wait_ge(S("v_tables"), o.n)
            v.memset(prod[0:NT, 0:1], 0.0)
            v.tensor_tensor(prod[0:NT, 1:GT], ohb[0:NT, 1:GT], ohb[0:NT, 0:GT - 1], ALU.mult)
            v.tensor_scalar(small[0:1, 2:3], small[0:1, 1:2], -1.0, 1.0, ALU.mult, ALU.add).then_inc(S("tables_ready"), 1)
            dve.wait_ge(S("tables_done"), 1)
            for h in range(2):
                v.tensor_copy(same[:, h * H:(h + 1) * H], psum[1 + h][:, 0:H])
                v.tensor_copy(a1t[:, h * H:(h + 1) * H], psum[3 + h][:, 0:H])
                v.tensor_scalar(bt_i[0:1, h * H:(h + 1) * H], psum[5 + h][0:1, 0:H], -float(TW), float((NT - 1) * TW),
                                ALU.mult, ALU.add)
            v.tensor_copy(shift[:, :], psum[0][:, 0:1])

        def steady(eng, step, lag):
            for i in range(RING):
                step(i, i, 0)
            with eng.Fori(1, NG // RING) as k:
                for j in range(RING):
                    step(k * RING + j, j, k)
            for i in range(NG // RING * RING, NG + lag):
                step(i, i % RING, i // RING)

        def live(i, lag, n=NG):
            return not isinstance(i, int) or 0 <= i - lag < n

        def gather_pool(pool):
            pool.wait_ge(S("records_in"), 16)

            def step(i, j, k):
                if live(i, 0):
                    if due((i - RING + 1) * G):
                        pool.wait_ge(S("product_done"), (i - RING + 1) * G)
                    pool.tensor_copy(idx_g[j][:, :], rec_all.rearrange("p (t c) -> p t c", c=2)[:, ds(i * G, G), 1])\
                        .then_inc(S("indices_ready"), 1)
                    pool.wait_ge(S("indices_ready"), i + 1)
                    pool.sem_inc(S("pool_steps"), 1)
                    for q in range(G):
                        pool.indirect_dma_start(rows_in[j][:, q * TW:(q + 1) * TW], None, table_d[:, :],
                                                bass.IndirectOffsetOnAxis(ap=idx_g[j][:, q:q + 1], axis=0))\
                            .then_inc(S(f"rows_in{j}"), 16)

            steady(pool, step, 0)

        def gather_tensor(pe):
            mm = nc.tensor.matmul

            def step(i, j, k):
                if live(i, 2):
                    b, t = j % 2, i - 2
                    pe.wait_ge(S("shift_ready"), t + 1)
                    pe.wait_ge(S("member_ready"), t + 1)
                    if due(t - 1):
                        pe.wait_ge(S("z_ready"), t - 1)
                    for q in range(G):
                        last = mm(psum[2 + b][:, 2 * q:2 * q + 2], member[b][:, q * P:(q + 1) * P], lb[b][:, q:q + G + 2:G + 1],
                                  start=True, stop=True)
                    last.then_inc(S("edge_done"), 1)
                if live(i, 4):
                    b, g, t = j % 2, (j - 4) % RING, i - 4
                    for q in range(G):
                        pe.wait_ge(S("weight_ready"), t * G + q + 1)
                        if due((t - 1) * G + q + 1):
                            pe.wait_ge(S("acc_done"), (t - 1) * G + q + 1)
                        mm(psum[4 + q][:, 0:C + 1], weight[b][:, q * P:(q + 1) * P], rows_in[g][:, q * TW:q * TW + C + 1],
                           start=True, stop=True).then_inc(S("product_done"), 1)
                if live(i, 0):
                    b = j % 2
                    if due(i - 1):
                        pe.wait_ge(S("member_ready"), i - 1)
                    for q in range(G):
                        pe.wait_ge(S("masked_ready"), i * G + q + 1)
                        last = nc.tensor.transpose(psum[b][:, q * P:(q + 1) * P], masked[j % 4][:, q * P:(q + 1) * P], ident[:, :])
                    last.then_inc(S("masked_turned"), 1)

            steady(pe, step, 4)

        def gather_scalar(act):
            a = nc.scalar.activation

            def step(i, j, k):
                if live(i, 3):
                    b, t = (j - 3) % 2, i - 3
                    act.wait_ge(S("z_ready"), t + 1)
                    if due(t - 1):
                        act.wait_ge(S("wscale_ready"), t - 1)
                    a(wexp[b][:, :], zarg[:, :], ACT.Exp).then_inc(S("wexp_ready"), 1)
                if live(i, 1):
                    b = (j - 1) % 2
                    act.wait_ge(S("max_done"), i)
                    if due(i - 2):
                        act.wait_ge(S("edge_done"), i - 2)
                    a(member[b][:, :], psum[b][:, :], ACT.Sign).then_inc(S("member_ready"), 1)
                if live(i, 3):
                    b, t = (j - 3) % 2, i - 3
                    act.wait_ge(S("wscale_ready"), t + 1)
                    if due((t - 1) * G):
                        act.wait_ge(S("product_done"), (t - 1) * G)
                    for q in range(G):
                        a(weight[b][:, q * P:(q + 1) * P], masked[(j - 3) % 4][:, q * P:(q + 1) * P], ACT.Copy,
                          scale=wscale[b][:, q:q + 1]).then_inc(S("weight_ready"), 1)
                if live(i, 1):
                    act.wait_ge(S("dm_ready"), i)
                    if due((i - RING) * G):
                        act.wait_ge(S("acc_done"), (i - RING) * G)
                    a(alpha[(j - 1) % RING][:, :], dm[:, :], ACT.Exp).then_inc(S("alpha_ready"), 1)

            steady(act, step, 3)

        def gather_vector(dve):
            v = nc.vector
            v.memset(nb[1][:, :], 0.0)
            v.memset(lb[1][:, :], 0.0)
            v.memset(acc[:, :], 0.0).then_inc(S("acc_cleared"), 1)
            dve.wait_ge(S("records_in"), 16)
            ra = rec_all.rearrange("p (t c) -> p t c", c=2)
            v.tensor_copy(lane_row[:, :], ra[:, :, 0]).then_inc(S("acc_cleared"), 1)
            dve.wait_ge(S("acc_cleared"), 2)

            def exponents(i, j, part):
                if not live(i, 3):
                    return
                b, t = (j - 3) % 2, i - 3
                pm = psum[2 + b][:, 0:2 * G].rearrange("p (q c) -> p q c", c=2)
                if part == 0:
                    gv = rows_in[(j - 3) % RING].rearrange("p (q c) -> p q c", c=TW)
                    dve.wait_ge(S("edge_done"), t + 1)
                    if due(t):
                        dve.wait_ge(S("wexp_ready"), t)
                    v.tensor_tensor(score[:, :], pm[:, :, 0], gv[:, :, C + 1], ALU.add).then_inc(S("z_steps"), 1)
                elif part == 1:
                    dve.wait_ge(S("z_steps"), t * 2 + 1)
                    v.scalar_tensor_tensor(leaky[:, :], score[:, :], SLOPE, score[:, :], ALU.mult, ALU.max).then_inc(S("z_steps"), 1)
                else:
                    dve.wait_ge(S("z_steps"), t * 2 + 2)
                    v.tensor_tensor(zarg[:, :], leaky[:, :], pm[:, :, 1], ALU.subtract).then_inc(S("z_ready"), 1)

            def add(i, j, q, columns):
                if not live(i, 4):
                    return
                t = i - 4
                if q == 0:
                    dve.wait_ge(S("alpha_ready"), t + 1)
                dve.wait_ge(S("product_done"), t * G + q + 1)
                if due(t * G + q):
                    dve.wait_ge(S("acc_done"), t * G + q)
                here = acc[:, bass.ds(columns[q], C + 1)]
                v.scalar_tensor_tensor(here, here, alpha[(j - 4) % RING][:, q:q + 1], psum[4 + q][:, 0:C + 1],
                                       ALU.mult, ALU.add).then_inc(S("acc_done"), 1)

            def mask(i, j, q):
                if live(i, 0):
                    v.tensor_scalar(masked[j % 4][:, q * P:(q + 1) * P], iota[:, :], lane_row[:, ds(i * G + q)],
                                    a2s[j % 2][:, q:q + 1], ALU.is_equal, ALU.mult).then_inc(S("masked_ready"), 1)

            def step(i, j, k):
                columns = None
                exponents(i, j, 0)
                if live(i, 0):
                    b = j % 2
                    dve.wait_ge(S(f"rows_in{j}"), k * (16 * G) + 16 * G)
                    if due(i - 1):
                        dve.wait_ge(S("masked_ready"), (i - 1) * G)
                    gv = rows_in[j].rearrange("p (q c) -> p q c", c=TW)
                    v.tensor_scalar(a2s[b][:, :], gv[:, :, C + 1], shift[:, :], 0.5, ALU.add, ALU.max).then_inc(S("a2s_ready"), 1)
                exponents(i, j, 1)
                if live(i, 0):
                    dve.wait_ge(S("a2s_ready"), i + 1)
                    if due(i - 3):
                        dve.wait_ge(S("wscale_ready"), i - 3)
                    v.reciprocal(rec_a2[j % 4][:, :], a2s[b][:, :])
                exponents(i, j, 2)
                if live(i, 1):
                    b, t = (j - 1) % 2, i - 1
                    if due(t - 1):
                        dve.wait_ge(S("edge_done"), t - 1)
                    v.tensor_copy(lb[b][:, 0:G], a1t[:, ds(t * G, G)])
                    if due(t):
                        dve.wait_ge(S("shift_ready"), t)
                    if due(t - 1):
                        dve.wait_ge(S("dm_steps"), t - 1)
                    v.tensor_copy(lb[b][:, G:G + 1], lb[1 - b][:, 2 * G:2 * G + 1])
                    dve.wait_ge(S("masked_turned"), t + 1)
                    if due(t):
                        dve.wait_ge(S("nb_steps"), t)
                    v.tensor_reduce(tile_max[:, :], psum[b].rearrange("p (q r) -> p q r", q=G)[:, :, :], AX.X, ALU.max)\
                        .then_inc(S("max_done"), 1)
                if live(i, 4):
                    _, columns = nc.values_load_multi_w_load_instructions(
                        bt_i[0:1, ds((i - 4) * G, G)], engines=(dve.engine,), min_val=0, max_val=(NT - 1) * TW,
                        skip_runtime_bounds_check_because="the table holds first columns of buckets")
                if live(i, 3):
                    b, t = (j - 3) % 2, i - 3
                    dve.wait_ge(S("wexp_ready"), t + 1)
                    if due((t - 1) * G):
                        dve.wait_ge(S("weight_ready"), (t - 1) * G)
                    v.tensor_tensor(wscale[b][:, :], wexp[b][:, :], rec_a2[(j - 3) % 4][:, :], ALU.mult).then_inc(S("wscale_ready"), 1)
                if live(i, 0):
                    if due(i - 3):
                        dve.wait_ge(S("masked_turned"), i - 3)
                    if due((i - 3) * G):
                        dve.wait_ge(S("weight_ready"), (i - 3) * G)
                b, t = (j - 1) % 2, i - 1
                for q in range(G):
                    mask(i, j, q)
                    if live(i, 1):
                        if q == 0:
                            dve.wait_ge(S("max_done"), t + 1)
                            if due(t):
                                dve.wait_ge(S("lin_steps"), t)
                            v.tensor_tensor_scan(nb[b][:, :], same[:, ds(t * G, G)], tile_max[:, :], nb[1 - b][:, G - 1:G],
                                                 ALU.mult, ALU.max).then_inc(S("nb_steps"), 1)
                        elif q == 1:
                            dve.wait_ge(S("nb_steps"), t + 1)
                            if due(t):
                                dve.wait_ge(S("shift_ready"), t)
                            v.scalar_tensor_tensor(lin[:, :], nb[b][:, :], shift[:, :], a1t[:, ds(t * G, G)],
                                                   ALU.subtract, ALU.add).then_inc(S("lin_steps"), 1)
                        elif q == 2:
                            dve.wait_ge(S("lin_steps"), t + 1)
                            v.scalar_tensor_tensor(lb[b][:, G + 1:2 * G + 1], lin[:, :], SLOPE, lin[:, :], ALU.mult, ALU.max)\
                                .then_inc(S("shift_ready"), 1)
                        else:
                            dve.wait_ge(S("shift_ready"), t + 1)
                            if due(t):
                                dve.wait_ge(S("dm_ready"), t)
                            v.tensor_tensor(dm0[:, :], lb[b][:, G:2 * G], lb[b][:, G + 1:2 * G + 1], ALU.subtract)\
                                .then_inc(S("dm_steps"), 1)
                    add(i, j, q, columns)
                if live(i, 1):
                    dve.wait_ge(S("dm_steps"), t + 1)
                    if due(t):
                        dve.wait_ge(S("alpha_ready"), t)
                    v.tensor_tensor(dm[:, :], dm0[:, :], same[:, ds(t * G, G)], ALU.mult).then_inc(S("dm_ready"), 1)

            steady(dve, step, 4)

        def pairs(eng, step, lag, n=NT):
            step(0, 0)
            step(1, 1)
            with eng.Fori(1, n // 2) as k:
                step(k * 2, 0)
                step(k * 2 + 1, 1)
            for i in range(n, n + lag):
                step(i, i % 2)

        def route_sync(sp):
            sp.dma_start(w2_sb[:, :], w2).then_inc(S("w2_in"), 16)
            sp.dma_start(w13_sb[:, (NE - 1) * 4 * F:], w13[:, (NE - 1) * 4 * F:]).then_inc(S("w13_in"), 16)
            sp.dma_start(router.rearrange("p (k n) -> p k n", k=2), w_router.rearrange("(k p) n -> p k n", p=P))\
                .then_inc(S("router_in"), 16)

            def step1(i, b):
                if live(i, 0, NT):
                    if due(i - 1):
                        sp.wait_ge(S("x2_ready"), after("x2_ready", i - 1))
                    sp.dma_start(b2[b][:, :], tile_of(base2_d, i)).then_inc(S(f"b2_in{b}"), 16)
                if live(i, 1, NT):
                    if due(i):
                        sp.wait_ge(S("x2_ready"), after("x2_ready", i))
                    sp.dma_start(tile_of(x2_d, i - 1), acc[:, bass.ds((i - 1) * TW, C)] if not isinstance(i, int)
                                 else acc[:, (i - 1) * TW:(i - 1) * TW + C]).then_inc(S("x2_out"), 16)

            pairs(sp, step1, 1)

            def step2(i, b):
                sp.wait_ge(S("xn2_ready"), after("xn2_ready", i + 1))
                sp.dma_start(tile_of(xn2_d, i), xn2[b][:, :]).then_inc(S(f"xn2_out{b}"), 16)

            pairs(sp, step2, 0)
            sp.wait_ge(S("x2_out"), 16 * NT)
            sp.wait_ge(S("xn2_out0"), after("xn2_out0", 8 * NT))
            sp.wait_ge(S("xn2_out1"), after("xn2_out1", 8 * NT))

        def route_tensor(pe):
            mm = nc.tensor.matmul
            pe.wait_ge(S("router_in"), 16)

            def step(i, b):
                if live(i, 0, NT):
                    pe.wait_ge(S("xn2_ready"), after("xn2_ready", i + 1))
                    if due(i - 1):
                        pe.wait_ge(S("xn2t_ready"), after("xn2t_ready", i - 1))
                    nc.tensor.transpose(psum[b][:, 0:P], xn2[b][:, 0:P], ident[:, :])
                    nc.tensor.transpose(psum[b][:, P:C], xn2[b][:, P:C], ident[:, :]).then_inc(S("xn2_turned"), 1)
                if live(i, 1, NT):
                    if due(i):
                        pe.wait_ge(S("xn2t_ready"), after("xn2t_ready", i))
                    if due(i - 2):
                        pe.wait_ge(S("logits_ready"), after("logits_ready", i - 2))
                    for c in range(2):
                        last = mm(psum[3 - b][:, 0:NE], xn2t[1 - b][:, c * P:(c + 1) * P], router[:, c * NE:(c + 1) * NE],
                                  start=(c == 0), stop=(c == 1))
                    last.then_inc(S("logits_done"), 1)

            pairs(pe, step, 1)
            pe.wait_ge(S("totals_ready"), 1)
            mm(psum[4][:, 0:NE], ones[:, :], tot[:, :], start=True, stop=True)
            mm(psum[4][:, NE:2 * NE], before[:, :], tot[:, :], start=True, stop=True).then_inc(S("totals_done"), 1)

        def route_scalar(act):
            act.wait_ge(S("var2_ready"), 1)
            nc.scalar.activation(rstd2[:, :], rstd2[:, :], ACT.Sqrt).then_inc(S("std2_ready"), 1)

            def step(i, b):
                act.wait_ge(S("xn2_turned"), i + 1)
                if due(i - 1):
                    act.wait_ge(S("logits_done"), after("logits_done", i - 1))
                nc.scalar.activation(xn2t[b][:, :], psum[b][:, 0:C], ACT.Copy).then_inc(S("xn2t_ready"), 1)

            pairs(act, step, 0)
            act.wait_ge(S("exponents_ready"), 1)
            nc.scalar.activation(scr[:, 0:NT * NE], scr[:, 0:NT * NE], ACT.Exp)
            nc.scalar.activation(pz[:, 0:NT], pz[:, 0:NT], ACT.Exp).then_inc(S("exps_ready"), 1)

        def route_vector(dve):
            v = nc.vector
            o = Order(dve, "v_route")
            den = acc.rearrange("p (t c) -> p t c", c=TW)[:, :, C]
            o(v.tensor_scalar(rden[:, :], den, 1e-30, None, ALU.max))
            dve.wait_ge(S("v_route"), o.n)
            o(v.reciprocal(rden[:, :], rden[:, :]))
            dve.wait_ge(S("v_route"), o.n)

            def step1(i, b):
                here = acc[:, ds(i * TW, C)]
                dve.wait_ge(S(f"b2_in{b}"), after(f"b2_in{b}", (i - b) * 8 + 16))
                v.scalar_tensor_tensor(here, here, rden[:, ds(i)], b2[b][:, :], ALU.mult, ALU.add).then_inc(S("x2_ready"), 1)
                dve.wait_ge(S("x2_ready"), after("x2_ready", i + 1))
                if due(i):
                    dve.wait_ge(S("mv_ready"), after("mv_ready", i))
                dve.sem_inc(S("vector_steps"), 1)
                v.bn_stats(st2[:, :], here).then_inc(S("mv_steps"), 1)
                dve.wait_ge(S("mv_steps"), i * 2 + 1)
                dve.sem_inc(S("vector_steps"), 1)
                v.bn_aggr(mvt[:, :], st2[:, :]).then_inc(S("mv_steps"), 1)
                dve.wait_ge(S("mv_steps"), i * 2 + 2)
                v.tensor_copy(mv2[:, ds(i * 2, 2)], mvt[:, :]).then_inc(S("mv_ready"), 1)

            pairs(dve, step1, 0)
            dve.wait_ge(S("mv_ready"), after("mv_ready", NT))
            mvv = mv2.rearrange("p (t c) -> p t c", c=2)
            v.tensor_scalar(rstd2[:, :], mvv[:, :, 1], EPS, None, ALU.add).then_inc(S("var2_ready"), 1)
            dve.wait_ge(S("std2_ready"), 1)
            o(v.reciprocal(rstd2[:, :], rstd2[:, :]))
            dve.wait_ge(S("v_route"), o.n)

            def step2(i, b):
                if live(i, 0, NT):
                    if not (isinstance(i, int) and i < 2):
                        if due((i - b) * 8):
                            dve.wait_ge(S(f"xn2_out{b}"), after(f"xn2_out{b}", (i - b) * 8))
                    if due(i - 1):
                        dve.wait_ge(S("xn2_turned"), i - 1)
                    v.tensor_scalar(xn2[b][:, :], acc[:, ds(i * TW, C)], mv2[:, ds(i * 2)], rstd2[:, ds(i)],
                                    ALU.subtract, ALU.mult).then_inc(S("xn2_ready"), 1)
                if live(i, 1, NT):
                    if due(i):
                        dve.wait_ge(S("logits_done"), after("logits_done", i))
                    v.tensor_copy(logits[:, ds((i - 1) * NE, NE)], psum[3 - b][:, 0:NE]).then_inc(S("logits_ready"), 1)

            pairs(dve, step2, 1)
            dve.wait_ge(S("logits_ready"), after("logits_ready", NT))
            dve.wait_ge(S("xn2_ready"), after("xn2_ready", NT))
            dve.wait_ge(S("x2_out"), 16 * NT)

            def step(ins):
                o(ins)
                dve.wait_ge(S("v_route"), o.n)
            L3 = logits.rearrange("p (t e) -> p t e", e=NE)
            O1 = oh12[:, 0:NT * NE].rearrange("p (t e) -> p t e", e=NE)
            O2 = oh12[:, NT * NE:2 * NT * NE].rearrange("p (t e) -> p t e", e=NE)
            S3 = scr[:, 0:NT * NE].rearrange("p (t e) -> p t e", e=NE)
            S4 = scr[:, NT * NE:2 * NT * NE].rearrange("p (t e) -> p t e", e=NE)
            nb3 = nidx.unsqueeze(1).to_broadcast([P, NT, NE])

            def bc(ap):
                return ap.unsqueeze(2).to_broadcast([P, NT, NE])
            step(v.tensor_scalar(nidx[:, :], iota[:, 0:NE], -1.0, float(NE), ALU.mult, ALU.add))
            for k, (src_, hot) in enumerate(((L3, O1), (S4, O2))):
                tk = top[:, k * NT:(k + 1) * NT]
                step(v.tensor_reduce(tk, src_, AX.X, ALU.max))
                step(v.tensor_tensor(S3, src_, bc(tk), ALU.is_equal))
                step(v.tensor_tensor(S3, S3, nb3, ALU.mult))
                step(v.tensor_reduce(ti[:, :], S3, AX.X, ALU.max))
                step(v.tensor_tensor(hot, nb3, bc(ti[:, :]), ALU.is_equal))
                if k == 0:
                    step(v.scalar_tensor_tensor(scr[:, NT * NE:2 * NT * NE], oh12[:, 0:NT * NE], -3e38, logits[:, :],
                                                ALU.mult, ALU.add))
            o(v.tensor_tensor(S3, L3, bc(top[:, 0:NT]), ALU.subtract))
            v.tensor_tensor(pz[:, 0:NT], top[:, NT:2 * NT], top[:, 0:NT], ALU.subtract).then_inc(S("exponents_ready"), 1)
            dve.wait_ge(S("exps_ready"), 1)
            step(v.tensor_reduce(pz[:, NT:2 * NT], S3, AX.X, ALU.add))
            step(v.reciprocal(pz[:, NT:2 * NT], pz[:, NT:2 * NT]))
            step(v.tensor_tensor(pz[:, 2 * NT:3 * NT], pz[:, 0:NT], pz[:, NT:2 * NT], ALU.mult))
            step(v.scalar_tensor_tensor(pz[:, 3 * NT:4 * NT], pz[:, NT:2 * NT], 1e-9, pz[:, 2 * NT:3 * NT], ALU.add, ALU.add))
            step(v.reciprocal(pz[:, 3 * NT:4 * NT], pz[:, 3 * NT:4 * NT]))
            step(v.tensor_tensor(gate[:, 0:NT], pz[:, NT:2 * NT], pz[:, 3 * NT:4 * NT], ALU.mult))
            step(v.tensor_tensor(gate[:, NT:2 * NT], pz[:, 2 * NT:3 * NT], pz[:, 3 * NT:4 * NT], ALU.mult))
            for hot in (O1, O2):
                step(v.tensor_tensor(hot, hot, bc(valid[:, :]), ALU.mult))
            step(v.tensor_copy(pre_a[:, :], oh12[:, :]))
            bufs, d = [pre_a, pre_b], 1
            while d < 2 * NT:
                a_, b_ = bufs
                w = d * NE
                step(v.tensor_copy(b_[:, 0:w], a_[:, 0:w]))
                step(v.tensor_tensor(b_[:, w:], a_[:, w:], a_[:, 0:2 * NT * NE - w], ALU.add))
                bufs, d = [b_, a_], 2 * d
            incl = bufs[0]
            v.tensor_copy(tot[:, :], incl[:, (2 * NT - 1) * NE:2 * NT * NE]).then_inc(S("totals_ready"), 1)
            step(v.tensor_tensor(scr[:, :], incl[:, :], oh12[:, :], ALU.subtract))
            dve.wait_ge(S("totals_done"), 1)
            step(v.tensor_scalar(etile_i[:, :], psum[4][:, 0:NE], float(P - 1), None, ALU.add))
            step(v.tensor_scalar(etile_i[:, :], etile_i[:, :], 7, None, ALU.logical_shift_right))
            step(v.memset(escan[:, :], 0.0))
            W = 2 * NE
            step(v.tensor_copy(escan[:, NE:W], etile_i[:, :]))
            cur = 0
            for d in (1, 2, 4):
                a_, b_ = cur * W, (1 - cur) * W
                step(v.tensor_tensor(escan[:, b_ + NE:b_ + W], escan[:, a_ + NE:a_ + W], escan[:, a_ + NE - d:a_ + W - d], ALU.add))
                cur = 1 - cur
            step(v.tensor_copy(eend[:, :], escan[:, cur * W + NE:cur * W + W]))
            step(v.tensor_tensor(efirst[:, :], eend[:, :], etile_i[:, :], ALU.subtract))
            step(v.scalar_tensor_tensor(ebase[:, :], efirst[:, :], float(P), psum[4][:, NE:2 * NE], ALU.mult, ALU.add))
            R3v = scr.rearrange("p (t e) -> p t e", e=NE)
            step(v.tensor_tensor(R3v, R3v, ebase.unsqueeze(1).to_broadcast([P, 2 * NT, NE]), ALU.add))
            step(v.tensor_tensor(scr[:, :], scr[:, :], oh12[:, :], ALU.mult))
            step(v.tensor_reduce(pos_f[:, :], R3v, AX.X, ALU.add))
            step(v.tensor_copy(pos_i[:, :], pos_f[:, :]))
            T3 = tcmp.rearrange("p (t e) -> p t e", e=NE)
            step(v.tensor_tensor(T3, iota.unsqueeze(2).to_broadcast([P, P, NE]), eend.unsqueeze(1).to_broadcast([P, P, NE]), ALU.is_ge))
            step(v.tensor_reduce(ecount[:, :], T3, AX.X, ALU.add))
            step(v.tensor_scalar(et_i[:, :], ecount[:, :], float(NE - 1), None, ALU.min))

        NFULL = N // P

        def fours(eng, step, lag):
            for i in range(4):
                step(i, i)
            with eng.Fori(1, NFULL // 4) as k:
                for j in range(4):
                    step(k * 4 + j, j)
            for i in range(NFULL, NFULL + 1 + lag):
                step(i, i % 4)

        def lanes(i):
            return LAST_LANES if isinstance(i, int) and i == NFULL else P

        LAST_LANES = N - NFULL * P

        def dispatch_sync(sp):
            def step(i, j):
                if not (isinstance(i, int) and i < 4):
                    if due((i - j) * 8):
                        sp.wait_ge(S(f"sent{j}"), (i - j) * 8)
                sp.dma_start(xd[j][:, :], tile_of(xn2_d, i)).then_inc(S(f"xd_in{j}"), 16)

            fours(sp, step, 0)

        def slots_of(pool, i, j):
            pool.tensor_copy(idx_d[j][:, :], pos_i.rearrange("p (k t) -> p t k", k=2)[:, ds(i), :].rearrange("p a k -> p (a k)"))\
                .then_inc(S("slots_copied"), 1)

        def dispatch_pool(pool):
            def step(i, j):
                if not (isinstance(i, int) and i < 4):
                    if due((i - j) * 8):
                        pool.wait_ge(S(f"sent{j}"), (i - j) * 8)
                slots_of(pool, i, j)
                pool.wait_ge(S("slots_copied"), i + 1)
                pool.wait_ge(S(f"xd_in{j}"), (i - j) * 4 + 16)
                pool.sem_inc(S("pool_steps"), 1)
                n = lanes(i)
                for k in range(2):
                    pool.indirect_dma_start(xs_d[:, :], bass.IndirectOffsetOnAxis(ap=idx_d[j][0:n, k:k + 1], axis=0),
                                            xd[j][0:n, :], None).then_inc(S(f"sent{j}"), 16)

            fours(pool, step, 0)
            for j in range(4):
                pool.wait_ge(S(f"sent{j}"), 32 * len(range(j, NFULL + 1, 4)))

        def experts_sync(sp):
            def step(i, b):
                if live(i, 0, MT):
                    if due(i - 1):
                        sp.wait_ge(S("xs_turned"), after("xs_turned", i - 1))
                    sp.dma_start(xs[b][:, :], tile_of(xs_d.rearrange("(t p) c -> t p c", p=P), i)).then_inc(S(f"xs_in{b}"), 16)
                if live(i, 2, MT):
                    if due(i - 1):
                        sp.wait_ge(S("yo_ready"), after("yo_ready", i - 1))
                    sp.dma_start(tile_of(ys_d.rearrange("(t p) c -> t p c", p=P), i - 2), yo[b][:, :]).then_inc(S(f"yo_out{b}"), 16)

            pairs(sp, step, 2, MT)
            sp.wait_ge(S("yo_out0"), after("yo_out0", 8 * MT))
            sp.wait_ge(S("yo_out1"), after("yo_out1", 8 * MT))

        def experts_tensor(pe):
            mm = nc.tensor.matmul
            pe.wait_ge(S("w13_in"), 16 * NE)
            pe.wait_ge(S("w2_in"), 16)

            def turn(i, b):
                pe.wait_ge(S(f"xs_in{b}"), after(f"xs_in{b}", (i - b) * 8 + 16))
                if due(i):
                    pe.wait_ge(S("xst_ready"), after("xst_ready", i))
                nc.tensor.transpose(psum[0][:, 0:P], xs[b][:, 0:P], ident[:, :])
                nc.tensor.transpose(psum[0][:, P:C], xs[b][:, P:C], ident[:, :]).then_inc(S("xs_turned"), 1)

            def hidden(i, b, h, e):
                if due(i):
                    pe.wait_ge(S(f"gg{h}_ready"), after(f"gg{h}_ready", i))
                for m in range(2):
                    for c in range(2):
                        last = mm(psum[1 + 2 * h + m][:, 0:FH], xst[b][:, c * P:(c + 1) * P],
                                  w13_sb[:, bass.ds(e * (4 * F) + (c * 2 * F + m * F + h * FH), FH)],
                                  start=(c == 0), stop=(c == 1))
                last.then_inc(S(f"hidden{h}_done"), 1)

            def step(i, b):
                if live(i, 0, MT):
                    if isinstance(i, int) and i == 0:
                        turn(0, 0)
                    e = pe.value_load(et_i[0:1, ds(i)], min_val=0, max_val=NE - 1)
                    pe.wait_ge(S("xst_ready"), after("xst_ready", i + 1))
                    hidden(i, b, 0, e)
                if live(i, 1, MT):
                    if due(i):
                        pe.wait_ge(S("gg1_ready"), after("gg1_ready", i))
                    if due(i - 1):
                        pe.wait_ge(S("ggt_ready"), i - 1)
                    for c in range(4):
                        nc.tensor.transpose(psum[5][:, c * P:(c + 1) * P], gg[1 - b][:, c * P:(c + 1) * P], ident[:, :])
                    nc.tensor.transpose(psum[6][:, 0:P], gg[1 - b][:, 4 * P:5 * P], ident[:, :])
                    nc.tensor.transpose(psum[6][0:FL, P:2 * P], gg[1 - b][:, 5 * P:F], ident[:, :]).then_inc(S("gg_turned"), 1)
                if live(i, 0, MT):
                    hidden(i, b, 1, e)
                    if not isinstance(i, int) or i + 1 < MT:
                        turn(i + 1, 1 - b)
                if live(i, 1, MT):
                    e1 = pe.value_load(et_i[0:1, ds(i - 1)], min_val=0, max_val=NE - 1)
                    if due(i):
                        pe.wait_ge(S("ggt_ready"), i)
                    if due(i - 1):
                        pe.wait_ge(S("yo_ready"), after("yo_ready", i - 1))
                    for c in range(FC):
                        n = P if c < FC - 1 else FL
                        last = mm(psum[7][:, 0:C], ggt[1 - b][0:n, c * P:(c + 1) * P],
                                  w2_sb[0:n, bass.ds(e1 * (FC * C) + c * C, C)], start=(c == 0), stop=(c == FC - 1))
                    last.then_inc(S("y_done"), 1)

            step(0, 0)
            step(1, 1)
            with pe.Fori(1, MT // 2 - 1) as k:
                step(k * 2, 0)
                step(k * 2 + 1, 1)
            for i in range(MT - 2, MT + 1):
                step(i, i % 2)

        def experts_scalar(act):
            a = nc.scalar.activation

            def step(i, b):
                if live(i, 0, MT):
                    if isinstance(i, int) and i == 0:
                        act.wait_ge(S("xs_turned"), after("xs_turned", 1))
                        a(xst[0][:, :], psum[0][:, 0:C], ACT.Copy).then_inc(S("xst_ready"), 1)
                    act.wait_ge(S("hidden0_done"), after("hidden0_done", i + 1))
                    if due(i):
                        act.wait_ge(S("gg0_ready"), after("gg0_ready", i))
                    a(sig[0][:, :], psum[1][:, 0:FH], ACT.Sigmoid).then_inc(S("sig0_ready"), 1)
                if live(i, 1, MT):
                    if due(i):
                        act.wait_ge(S("gg_turned"), after("gg_turned", i))
                    if due(i - 2):
                        act.wait_ge(S("y_done"), after("y_done", i - 2))
                    a(ggt[1 - b][:, 0:4 * P], psum[5][:, :], ACT.Copy)
                    a(ggt[1 - b][:, 4 * P:5 * P], psum[6][:, 0:P], ACT.Copy)
                    a(ggt[1 - b][0:FL, 5 * P:6 * P], psum[6][0:FL, P:2 * P], ACT.Copy).then_inc(S("ggt_ready"), 1)
                if live(i, 0, MT):
                    act.wait_ge(S("hidden1_done"), after("hidden1_done", i + 1))
                    if due(i):
                        act.wait_ge(S("gg1_ready"), after("gg1_ready", i))
                    a(sig[1][:, :], psum[3][:, 0:FH], ACT.Sigmoid).then_inc(S("sig1_ready"), 1)
                    if not isinstance(i, int) or i + 1 < MT:
                        act.wait_ge(S("xs_turned"), after("xs_turned", i + 2))
                        if due(i):
                            act.wait_ge(S("hidden1_done"), after("hidden1_done", i))
                        a(xst[1 - b][:, :], psum[0][:, 0:C], ACT.Copy).then_inc(S("xst_ready"), 1)
                if live(i, 1, MT):
                    if due(i):
                        act.wait_ge(S("y_done"), after("y_done", i))
                    if not (isinstance(i, int) and i - 1 < 2):
                        if due((i - 1 - (1 - b)) * 8):
                            act.wait_ge(S(f"yo_out{1 - b}"), after(f"yo_out{1 - b}", (i - 1 - (1 - b)) * 8))
                    a(yo[1 - b][:, :], psum[7][:, 0:C], ACT.Copy).then_inc(S("yo_ready"), 1)

            step(0, 0)
            step(1, 1)
            with act.Fori(1, MT // 2 - 1) as k:
                step(k * 2, 0)
                step(k * 2 + 1, 1)
            for i in range(MT - 2, MT + 1):
                step(i, i % 2)

        def experts_vector(dve):
            v = nc.vector

            def step(i, b):
                for h in range(2):
                    dve.wait_ge(S(f"sig{h}_ready"), after(f"sig{h}_ready", i + 1))
                    if due(i):
                        dve.wait_ge(S(f"gg{h}_ready"), after(f"gg{h}_ready", i))
                    v.tensor_tensor(prod1[h][:, :], psum[1 + 2 * h][:, 0:FH], sig[h][:, :], ALU.mult).then_inc(S(f"silu{h}"), 1)
                    dve.wait_ge(S(f"silu{h}"), i + 1)
                    if due(i - 1):
                        dve.wait_ge(S("gg_turned"), after("gg_turned", i - 1))
                    v.tensor_tensor(gg[b][:, h * FH:(h + 1) * FH], psum[2 + 2 * h][:, 0:FH], prod1[h][:, :], ALU.mult)\
                        .then_inc(S(f"gg{h}_ready"), 1)

            pairs(dve, step, 0, MT)

        def combine_pool(pool):
            def step(i, j):
                if not (isinstance(i, int) and i < 4):
                    if due(i - 3):
                        pool.wait_ge(S("sum_ready"), after("sum_ready", i - 3))
                slots_of(pool, i, j)
                pool.wait_ge(S("slots_copied"), i + 1 + NFULL + 1)
                pool.sem_inc(S("pool_steps"), 1)
                n = lanes(i)
                for k, y in enumerate((y1, y2)):
                    pool.indirect_dma_start(y[j][0:n, :], None, ys_d[:, :],
                                            bass.IndirectOffsetOnAxis(ap=idx_d[j][0:n, k:k + 1], axis=0)).then_inc(S(f"y_in{j}"), 16)

            fours(pool, step, 0)

        def combine_sync(sp):
            def step(i, j):
                if live(i, 0, NFULL + 1):
                    if not (isinstance(i, int) and i < 4):
                        if due((i - j) * 4):
                            sp.wait_ge(S(f"out_done{j}"), (i - j) * 4)
                    sp.dma_start(xd[j][:, :], tile_of(x2_d, i)).then_inc(S(f"x2_in{j}"), 16)
                if live(i, 2, NFULL + 1):
                    n = lanes(i - 2) if isinstance(i, int) else P
                    if due(i - 1):
                        sp.wait_ge(S("sum_ready"), after("sum_ready", i - 1))
                    row = (i - 2) * P
                    sp.dma_start(out[ds(row, n), :], xd[(j - 2) % 4][0:n, :]).then_inc(S(f"out_done{(j - 2) % 4}"), 16)

            fours(sp, step, 2)
            for j in range(4):
                sp.wait_ge(S(f"out_done{j}"), 16 * len(range(j, NFULL + 1, 4)))

        def combine_vector(dve):
            v = nc.vector

            def step(i, j):
                n = lanes(i)
                dve.wait_ge(S(f"y_in{j}"), after(f"y_in{j}", (i - j) * 8 + 32))
                dve.wait_ge(S(f"x2_in{j}"), after(f"x2_in{j}", (i - j) * 4 + 16))
                v.scalar_tensor_tensor(xd[j][0:n, :], y1[j][0:n, :], gate[0:n, ds(i)], xd[j][0:n, :], ALU.mult, ALU.add)\
                    .then_inc(S("half_sum"), 1)
                dve.wait_ge(S("half_sum"), i + 1)
                v.scalar_tensor_tensor(xd[j][0:n, :], y2[j][0:n, :], gate[0:n, ds(i + NT)], xd[j][0:n, :], ALU.mult, ALU.add)\
                    .then_inc(S("sum_ready"), 1)

            fours(dve, step, 0)

        def sort_pool(pool):
            pool.iota(iota_i[:, :], pattern=[[1, P]], base=0, channel_multiplier=0).then_inc(S("iota_ready"), 1)
            pool.iota(tile_i[:, :], pattern=[[1, GT]], base=0, channel_multiplier=0)
            pool.iota(lane_i[:, :], pattern=[[P, NT]], base=0, channel_multiplier=1).then_inc(S("pool_lanes"), 1)
            pool.memset(ident[:, :], 0.0)
            pool.memset(before[:, :], 1.0).then_inc(S("pool_set"), 1)
            pool.wait_ge(S("pool_set"), 1)
            pool.affine_select(out=ident[:, :], in_=ident[:, :], compare_op=ALU.not_equal, fill=1.0, base=0,
                               pattern=[[-1, P]], channel_multiplier=1)
            pool.affine_select(out=before[:, :], in_=before[:, :], compare_op=ALU.is_gt, fill=0.0, base=0,
                               pattern=[[1, P]], channel_multiplier=-1).then_inc(S("consts_ready"), 1)
            pool.wait_ge(S("rec_cleared"), 16)

            def chunk(k, b):
                pool.wait_ge(S("slots_ready"), k + 1)
                if not (isinstance(k, int) and k < 2):
                    if due((k - b) * (8 * EC)):
                        pool.wait_ge(S(f"sort_scattered{b}"), (k - b) * (8 * EC))
                pool.tensor_copy(idx_ring[:, b * EC:(b + 1) * EC], slot_i[:, bass.ds(k * EC, EC)])
                pool.tensor_copy(rec_ring[:, b * 2 * EC:(b + 1) * 2 * EC],
                                 rec[:, bass.ds(k * (2 * EC), 2 * EC)]).then_inc(S("ring_filled"), 1)
                pool.wait_ge(S("ring_filled"), k + 1)
                pool.sem_inc(S("pool_steps"), 1)
                for j in range(EC):
                    r = b * EC + j
                    pool.indirect_dma_start(rec_d[:, :], bass.IndirectOffsetOnAxis(ap=idx_ring[:, r:r + 1], axis=0),
                                            rec_ring[:, 2 * r:2 * r + 2], None).then_inc(S(f"sort_scattered{b}"), 16)

            chunk(0, 0)
            chunk(1, 1)
            with pool.Fori(1, NCH // 2) as i:
                chunk(i * 2, 0)
                chunk(i * 2 + 1, 1)


        def sort_vector(dve):
            v = nc.vector
            o = Order(dve, "v_sort")
            v.memset(row_i[:, FULL:ET], 49 * P)
            v.memset(col_i[:, FULL:ET], DUMMY).then_inc(S("edges_cleared"), 1)
            ri = rec_init.rearrange("p (t c) -> p t c", c=2)
            v.memset(ri[:, :, 0], -1).then_inc(S("rec_init_ready"), 1)
            v.memset(ri[:, :, 1], DUMMY).then_inc(S("rec_init_ready"), 1)
            v.memset(ones[:, :], 1.0).then_inc(S("ones_ready"), 1)
            v.memset(zeros[:, :], 0.0).then_inc(S("zeros_ready"), 1)
            o(v.memset(scan[:, :], 0.0))
            dve.wait_ge(S("iota_ready"), 1)
            o(v.tensor_copy(iota[:, :], iota_i[:, :]))
            dve.wait_ge(S("edges_in"), 64)
            rc = rec.rearrange("p (t c) -> p t c", c=2)
            o(v.tensor_scalar(hi_i[:, :], row_i[:, :], 7, None, ALU.logical_shift_right))
            v.tensor_scalar(rc[:, :, 0], row_i[:, :], P - 1, None, ALU.bitwise_and)
            v.tensor_copy(rc[:, :, 1], col_i[:, :])
            dve.wait_ge(S("v_sort"), o.n)
            o(v.tensor_copy(hi_f[:, :], hi_i[:, :]))
            dve.wait_ge(S("v_sort"), o.n)
            with dve.Fori(0, NT) as i:
                v.tensor_scalar(mask[:, :], hi_f[:, :], iota[:, bass.ds(i, 1)], None, ALU.is_equal).then_inc(S("hist_mask"), 1)
                dve.wait_ge(S("hist_mask"), i + 1)
                v.tensor_reduce(hist[:, bass.ds(i, 1)], mask[:, :], AX.X, ALU.add).then_inc(S("hist_done"), 1)
                dve.wait_ge(S("hist_done"), i + 1)
            dve.wait_ge(S("hist_sums"), 1)
            o(v.tensor_scalar(tiles_i[:, :], psum[0][:, 0:NT], float(P - 1), None, ALU.add))
            dve.wait_ge(S("v_sort"), o.n)
            o(v.tensor_scalar(tiles_i[:, :], tiles_i[:, :], 7, None, ALU.logical_shift_right))
            dve.wait_ge(S("v_sort"), o.n)
            W = 64 + NT
            o(v.tensor_copy(scan[:, 64:W], tiles_i[:, :]))
            dve.wait_ge(S("v_sort"), o.n)
            cur = 0
            for d in (1, 2, 4, 8, 16, 32):
                a, b = cur * W, (1 - cur) * W
                o(v.tensor_tensor(scan[:, b + 64:b + W], scan[:, a + 64:a + W], scan[:, a + 64 - d:a + W - d], ALU.add))
                dve.wait_ge(S("v_sort"), o.n)
                cur = 1 - cur
            o(v.tensor_copy(first[:, NT:2 * NT], scan[:, cur * W + 64:cur * W + W]))
            o(v.tensor_tensor(first[:, 0:NT], scan[:, cur * W + 64:cur * W + W], tiles_i[:, :], ALU.subtract))
            dve.wait_ge(S("v_sort"), o.n)
            v.scalar_tensor_tensor(run[:, 0:NT], first[:, 0:NT], float(P), psum[0][:, 64:64 + NT], ALU.mult, ALU.add)\
                .then_inc(S("first_ready"), 1)
            dve.wait_ge(S("first_ready"), 1)
            oh = onehot.rearrange("p (t b) -> p t b", b=NT)
            with dve.Fori(0, NCH) as k:
                v.tensor_tensor(oh, hi_f[:, bass.ds(k * EC, EC)].unsqueeze(2).to_broadcast([P, EC, NT]),
                                iota[:, 0:NT].unsqueeze(1).to_broadcast([P, EC, NT]), ALU.is_equal).then_inc(S("chain"), 1)
                c = 1
                for j in range(EC):
                    a, b = (j % 2) * NT, (1 - j % 2) * NT
                    dve.wait_ge(S("chain"), k * (EC + 4) + c)
                    v.tensor_tensor_reduce(junk[:, :], oh[:, j, :], run[:, a:a + NT], 1.0, 0.0, ALU.mult, ALU.add,
                                           chunk_pos[:, j:j + 1])
                    v.tensor_tensor(run[:, b:b + NT], run[:, a:a + NT], oh[:, j, :], ALU.add).then_inc(S("chain"), 1)
                    c += 1
                dve.wait_ge(S("chain"), k * (EC + 4) + c)
                v.tensor_copy(chunk_i[:, 0:EC], chunk_pos[:, :]).then_inc(S("chain"), 1)
                dve.wait_ge(S("chain"), k * (EC + 4) + c + 1)
                v.tensor_scalar(chunk_i[:, EC:2 * EC], chunk_i[:, 0:EC], 7, None, ALU.logical_shift_right)
                v.tensor_scalar(chunk_i[:, 0:EC], chunk_i[:, 0:EC], P - 1, None, ALU.bitwise_and).then_inc(S("chain"), 1)
                dve.wait_ge(S("chain"), k * (EC + 4) + c + 2)
                v.scalar_tensor_tensor(slot_i[:, bass.ds(k * EC, EC)], chunk_i[:, 0:EC], float(GT), chunk_i[:, EC:2 * EC],
                                       ALU.mult, ALU.add).then_inc(S("slots_ready"), 1)
                dve.wait_ge(S("slots_ready"), k + 1)
                dve.sem_inc(S("chain"), 1)



        @block.sync
        def _(sp):
            sort_sync(sp)
            project_sync(sp)
            mix_sync(sp)
            sp.wait_ge(S("sort_scattered0"), 16 * EC * (NCH // 2))
            sp.wait_ge(S("sort_scattered1"), 16 * EC * (NCH // 2))
            phase(sp, 1)
            sp.dma_start(rec_all[:, :], rec_d.rearrange("(p t) c -> p (t c)", p=P)).then_inc(S("records_in"), 16)
            phase(sp, 2)
            route_sync(sp)
            phase(sp, 3)
            dispatch_sync(sp)
            phase(sp, 4)
            experts_sync(sp)
            phase(sp, 5)
            combine_sync(sp)

        @block.gpsimd
        def _(pool):
            sort_pool(pool)
            phase(pool, 1)
            gather_pool(pool)
            phase(pool, 2)
            phase(pool, 3)
            dispatch_pool(pool)
            phase(pool, 4)
            phase(pool, 5)
            combine_pool(pool)

        @block.vector
        def _(dve):
            sort_vector(dve)
            project_vector(dve)
            mix_vector(dve)
            tables_vector(dve)
            phase(dve, 1)
            gather_vector(dve)
            phase(dve, 2)
            route_vector(dve)
            phase(dve, 3)
            phase(dve, 4)
            experts_vector(dve)
            phase(dve, 5)
            combine_vector(dve)

        @block.tensor
        def _(pe):
            pe.wait_ge(S("consts_ready"), 1)
            pe.wait_ge(S("ones_ready"), 1)
            pe.wait_ge(S("hist_done"), NT)
            nc.tensor.matmul(psum[0][:, 0:NT], ones[:, :], hist[:, :], start=True, stop=True)
            nc.tensor.matmul(psum[0][:, 64:64 + NT], before[:, :], hist[:, :], start=True, stop=True).then_inc(S("hist_sums"), 1)
            pe.wait_ge(S("first_ready"), 1)
            project_tensor(pe)
            mix_tensor(pe)
            tables_tensor(pe)
            phase(pe, 1)
            gather_tensor(pe)
            phase(pe, 2)
            route_tensor(pe)
            phase(pe, 3)
            phase(pe, 4)
            experts_tensor(pe)
            phase(pe, 5)

        @block.scalar
        def _(act):
            project_scalar(act)
            mix_scalar(act)
            phase(act, 1)
            gather_scalar(act)
            phase(act, 2)
            route_scalar(act)
            phase(act, 3)
            phase(act, 4)
            experts_scalar(act)
            phase(act, 5)


def kernel(**inputs):
    import numpy as _np
    import concourse.bacc as _bacc
    from concourse import mybir as _mybir
    from concourse.bass_utils import run_bass_kernel_spmd as _run

    g = {k: _np.ascontiguousarray(v) for k, v in inputs.items()}
    pad = _np.zeros((NT * P, C), _np.float32)
    pad[0:N] = g["x"]
    w1, w3, w2 = g["L0_ffn_w1"], g["L0_ffn_w3"], g["L0_ffn_w2"]
    w13 = _np.concatenate([w1.transpose(2, 0, 1), w3.transpose(2, 0, 1)], 2)
    w13 = w13.reshape(2, P, NE, 2 * F).transpose(1, 2, 0, 3)
    w2p = _np.zeros((NE, FC * P, C), _np.float32)
    w2p[:, 0:F] = w2.transpose(0, 2, 1)
    w2p = w2p.reshape(NE, FC, P, C).transpose(2, 0, 1, 3)
    qkv = g["L0_mix_W_qkv"]
    named = {
        "x": pad, "src": g["src"], "dst": g["dst"],
        "w_h": g["L0_gnn_W_layer"], "w_hT": g["L0_gnn_W_layer"].T, "b_h": g["L0_gnn_b_layer"],
        "w_a": _np.concatenate([g["L0_gnn_w_a1"], g["L0_gnn_w_a2"]], 0).T,
        "b_a": _np.concatenate([g["L0_gnn_b_a1"], g["L0_gnn_b_a2"]], 0),
        "w_qkv": qkv, "w_vT": qkv[:, 2 * C:].T, "b_qkv": g["L0_mix_b_qkv"],
        "w_out": g["L0_mix_W_out"], "b_out": g["L0_mix_b_out"],
        "b_cols": _np.stack([g["L0_mix_b_qkv"][2 * C:2 * C + P], g["L0_mix_b_qkv"][2 * C + P:], g["L0_gnn_b_layer"][:P],
                             g["L0_gnn_b_layer"][P:]], 1),
        "w_router": g["L0_ffn_router_w"].T, "w13": w13.reshape(P, -1), "w2": w2p.reshape(P, -1),
    }
    nc = _bacc.Bacc("TRN2", target_bir_lowering=False, num_devices=1)
    arrays, args = {}, []
    for name, a in named.items():
        arrays[f"in_{name}"] = _np.ascontiguousarray(a)
        args.append(nc.dram_tensor(f"in_{name}", a.shape, _mybir.dt.from_np(a.dtype), kind="ExternalInput").ap())
    args.append(nc.dram_tensor("out", (N, C), F32, kind="ExternalOutput").ap())
    build(nc, *args)
    r = _run(nc, [arrays], core_ids=[0])
    return r.results[0]["out"]
```

```python
from contextlib import ExitStack

import concourse.bass as bass
from concourse import mybir

ALU = mybir.AluOpType
ACT = mybir.ActivationFunctionType
AX = mybir.AxisListType
F32 = mybir.dt.float32
I32 = mybir.dt.int32
BF16 = mybir.dt.bfloat16

P = 128
N = 6250
C = 256
E = 106250
NT = 50
LAST = N - 48 * P
FULL = E // P
TAIL = E - FULL * P
EC = 16
ET = -(-(FULL + 1) // (2 * EC)) * 2 * EC
NCH = ET // EC
GT = 880
G = 4
NG = GT // G
RING = 8
TW = C + 2
DUMMY = NT * P
F = 682
FH = F // 2
FC = 6
FL = F - 5 * P
NE = 8
LATE = 2
MT = 106
SLOPE = 0.01
EPS = 1e-5

def build(nc, x, src, dst, w_h, w_hT, b_h, w_a, b_a, w_qkv, w_vT, b_qkv, w_out, b_out, b_cols, w_router, w13, w2, out):
    assert (E + 49 * 127) // P + -(-(ET * P - E) // P) <= GT and (2 * N + NE * 127) // P <= MT
    ctx = ExitStack()
    with ctx:
        def sem(name):
            return ctx.enter_context(nc.semaphore(name))

        def bank(name):
            return ctx.enter_context(nc.psum_tensor(name, [P, 512], F32))

        def dram(name, shape, dt):
            return nc.dram_tensor(name, shape, dt).ap()

        rec_d = dram("edge_records", [P * GT, 2], I32)
        table_d = dram("table", [DUMMY + 1, TW], F32)
        mix_d = dram("mix_inputs", [NT, P, 2 * C], F32)
        q2t_d, base_d = mix_d[:, :, 0:C], mix_d[:, :, C:2 * C]
        xn2_d = dram("xn2", [NT, P, C], F32)
        xs_d = dram("expert_in", [MT * P, TW], F32)

        ACC_W, W2_W, W13_W = NT * TW, NE * FC * C, NE * 2 * 2 * F
        R1, R2, R3, R4 = 0, ACC_W, ACC_W + W2_W, ACC_W + W2_W + W13_W
        arena = ctx.enter_context(nc.sbuf_tensor("arena", [P, 52900], F32))
        at = {1: R1, 2: R2, 3: R3, 4: R4}
        ends = {1: R3, 2: R3, 3: R4, 4: 52900}

        def take(region, width, dt=F32, parts=P):
            a = at[region]
            at[region] += width
            assert at[region] <= ends[region], (region, dict(at))
            v = arena[0:parts, a:a + width]
            return v if dt == F32 else v.bitcast(dt)

        def restart(region):
            at[region] = {1: R1, 2: R2, 3: R3, 4: R4}[region]

        w13_sb = arena[:, R3:R4]
        ident, ones, before, iota = take(4, P), take(4, P), take(4, P), take(4, P)
        zeros = take(4, 2 * TW)
        iota_i = take(4, P, I32)
        a12 = take(4, 2 * NT)
        shift = take(4, 1)
        valid = take(4, NT)
        small = take(4, 64)
        gate = take(4, 2 * NT)
        pos_i = take(4, 2 * NT, I32)
        et_i = take(4, P, I32)
        router = take(4, 2 * NE)
        token_i = take(4, NT, I32)
        spare_i, spare = take(4, 1, I32), take(4, 1)
        row_i, col_i, hi_i = take(1, ET, I32), take(1, ET, I32), take(1, ET, I32)
        ohb, prod = arena[:, R1:R1 + GT], arena[:, R1 + GT:R1 + 2 * GT]
        rec = take(1, 2 * ET, I32)
        hi_f = take(1, ET)
        hi_b = take(1, ET // 2, BF16)
        mask = [take(1, ET // 2, BF16) for _ in range(2)]
        slot_i = take(1, ET, I32)
        onehot = take(1, EC * NT)
        chunk_pos = take(1, EC)
        chunk_i = take(1, 2 * EC, I32)
        run = take(1, 2 * NT)
        junk = take(1, NT)
        idx_ring = take(1, 2 * EC, I32)
        rec_ring = take(1, 4 * EC, I32)
        hist = take(1, NT)
        scan = take(1, 2 * (64 + NT))
        tiles_i = take(1, NT, I32)
        first = take(1, 2 * NT)
        edge = take(1, 2)
        bweight = take(1, 1)
        at[2] = at[1]
        rec_init = take(2, 2 * GT, I32)
        wcat = take(2, 2 * (4 * C + 2))
        wnat = take(2, 2 * C)
        wa_sb = take(2, 4)
        wvt_sb, wout_sb = take(2, 2 * C), take(2, 2 * C)
        bias = take(2, 4 * C + 2)
        at_p = at[2]

        psum = [bank(f"bank{i}") for i in range(8)]
        s = {}

        carry = {}
        for j in range(4):
            n = len(range(j, N // P + 1, 4))
            if j < 2:
                carry[f"added{j}"] = (f"sent{j}", 32 * n)
        for b in range(2):
            n = len(range(b, NT, 4))
            carry[f"mix_in{b}"] = (f"x_in{b}", 8 * NT)
            carry[f"xs_in{b}"] = (f"x_in{b}", 8 * NT + 16 * n)
            carry[f"xn2_out{b}"] = (f"row_out{b}", 24 * NT)
        for j in (2, 3):
            carry[f"mix_in{j}"] = (f"mix_in{j}", 0)
            carry[f"xn2_out{j}"] = (f"xn2_out{j}", 0)
        for new, old_, count in (("gg_turned", "xn2_turned", NT), ("logits_done", "q2t_done", NT), ("xn2t_ready", "xnt_ready", NT),
                                 ("y_done", "hv_done", NT), ("yo_ready", "q2_ready", NT), ("x2_ready", "xn_ready", NT),
                                 ("xst_ready", "kn2_ready", NT), ("logits_ready", "kn_ready", NT), ("xn2_ready", "qk_taken", NT),
                                 ("gg0_ready", "hv_taken", NT), ("gg1_ready", "base_ready", NT), 
                                 ("sig0_ready", "k2_ready", NT), ("sig1_ready", "q4_ready", NT), ("hidden0_done", "sums_done", NT),
                                 ("hidden1_done", "xnt_done", NT), ("xs_turned", "mix_done", NT)):
            carry[new] = (old_, count)

        def S(name):
            name = carry.get(name, (name, 0))[0]
            if name not in s:
                s[name] = sem(name)
            return s[name]

        def after(name, value):
            return value + carry[name][1]

        def due(value):
            return not isinstance(value, int) or value > 0

        class Order:

            def __init__(self, eng, name):
                self.eng, self.name, self.n = eng, name, 0

            def __call__(self, ins):
                self.n += 1
                ins.then_inc(S(self.name), 1)
                return ins

        def phase(eng, k):
            eng.drain().then_inc(S("stage_done"), 1)
            eng.wait_ge(S("stage_done"), 5 * k)

        QK, H0, VO0, A0 = 0, 2 * C, 3 * C, 4 * C
        wc = wcat.rearrange("p (k n) -> p k n", k=2)
        x_in = [take(2, C) for _ in range(2)]
        xn = [take(2, C) for _ in range(2)]
        xnt = [take(2, C) for _ in range(2)]
        qk = take(2, 2 * C)
        q2, q4, k2, kn, kn2 = (take(2, C) for _ in range(5))
        gt_sb = take(2, 2 * C)
        g1_row, bvo_row = take(2, C, parts=1), take(2, C, parts=1)
        hb = [take(2, TW) for _ in range(2)]
        base = [take(2, C) for _ in range(2)]
        q2t = [take(2, C) for _ in range(2)]
        b_col = take(2, 4)
        bo_row = take(2, C)
        mean_w = take(2, 8)
        lane_i = take(2, NT, I32)
        q2s, q4s, fac2 = (take(2, NT) for _ in range(3))
        fac = take(4, NT)
        st6, mv, rstd = take(2, 12), take(2, 2), take(2, 2)
        k2s, rk, rkv = take(2, 1), take(2, 1), take(2, 1)
        kscale = take(2, 2)
        kw_sb = take(4, 2 * C)

        a1_rows = take(2, P)
        a1t_at = at[4]
        a1t, same = take(4, GT), take(4, GT)
        bt_i = take(4, GT, I32)
        tile_f, tile_i = same, bt_i
        restart(2)
        acc = arena[:, R1:R1 + ACC_W]
        rec_all = take(2, 2 * GT, I32)
        lane_row = take(2, GT // 2, BF16)
        iota_b = take(2, P // 2, BF16)
        at[5], ends[5] = R3 + (NE - LATE) * 4 * F, R4
        rows_in = [take(2, G * TW) for _ in range(RING - 2)] + [take(5, G * TW) for _ in range(2)]
        hot = [take(5, G * P // 2, BF16) for _ in range(RING)]
        masked = [take(2, G * P) for _ in range(2)]
        member = [take(2, G * P) for _ in range(2)]
        weight = [take(2, G * P), take(5, G * P)]
        idx_g = [take(2, G, I32) for _ in range(RING)]
        a2s = [take(2, G) for _ in range(2)]
        tile_max = take(2, G)
        nb = [take(2, G) for _ in range(2)]
        lin = take(2, G)
        lb = [take(2, 2 * G + 1) for _ in range(2)]
        dm0, dm = take(2, G), take(2, G)
        alpha = [take(2, G) for _ in range(RING)]
        score, leaky, zarg = take(2, G), take(2, G), take(2, G)
        wexp = [take(2, G) for _ in range(2)]
        at[4] = a1t_at
        restart(2)
        mix_in = [take(2, 2 * C) for _ in range(4)]
        mix_q, mix_b = [m[:, 0:C] for m in mix_in], [m[:, C:2 * C] for m in mix_in]
        xn2 = [take(2, C) for _ in range(4)]
        xn2t = [take(2, C) for _ in range(2)]
        st2 = take(2, 6)
        mv2 = [take(2, 2) for _ in range(2)]
        std2 = [take(2, 2) for _ in range(2)]
        rden = take(2, NT)
        logits = take(4, NT * NE)
        restart(1)
        nidx = take(1, NE)
        oh12 = take(1, 2 * NT * NE)
        scr = take(1, 2 * NT * NE)
        pre_a = take(1, 2 * NT * NE)
        top = take(1, 2 * NT)
        ti = take(1, NT)
        pz = take(1, 4 * NT)
        escan = take(1, 2 * (NE + NE))
        etile_i = take(1, NE, I32)
        efirst, eend, ebase = take(1, NE), take(1, NE), take(1, NE)
        tot = take(1, NE)
        tcmp = take(1, P * NE)
        ecount = take(1, P)
        pos_f = take(1, 2 * NT)
        fields = take(1, 4 * NT)
        xd = [[take(1, TW) for _ in range(2)] for _ in range(4)]
        idx_d = [take(1, 2, I32) for _ in range(4)]
        restart(1)
        xs = [take(1, TW) for _ in range(2)]
        slot_gate = [take(1, 1) for _ in range(2)]
        unused = take(1, 1)
        slot_row = [take(1, 1, I32) for _ in range(2)]
        xst = [take(1, C) for _ in range(2)]
        sig = [take(1, FH) for _ in range(2)]
        prod1 = [take(1, FH) for _ in range(2)]
        gg = [take(1, F) for _ in range(2)]
        ggt = [take(1, FC * P) for _ in range(2)]
        yo = [take(1, C) for _ in range(2)]
        w2_sb = arena[:, R2:R3]

        def ds(i, n=1):
            return slice(i, i + n) if isinstance(i, int) else bass.ds(i, n)

        def tile_of(t, j):
            return t[j] if isinstance(j, int) else t[bass.ds(j, 1), :, :].rearrange("a p c -> (a p) c")

        block = ctx.enter_context(nc.Block())
        from_here = dict(at)

        row_src = src[0:FULL * P].rearrange("(p t) -> p t", p=P)
        col_src = dst[0:FULL * P].rearrange("(p t) -> p t", p=P)

        def sort_sync(sp):
            sp.wait_ge(S("edges_cleared"), 1)
            sp.dma_start(row_i[:, 0:FULL], row_src).then_inc(S("edges_in"), 16)
            sp.dma_start(col_i[:, 0:FULL], col_src).then_inc(S("edges_in"), 16)
            sp.dma_start(row_i[0:TAIL, FULL:FULL + 1], src[FULL * P:E].rearrange("(p o) -> p o", o=1)).then_inc(S("edges_in"), 16)
            sp.dma_start(col_i[0:TAIL, FULL:FULL + 1], dst[FULL * P:E].rearrange("(p o) -> p o", o=1)).then_inc(S("edges_in"), 16)
            for e in range(NE - LATE):
                sp.dma_start(w13_sb[:, e * 4 * F:(e + 1) * 4 * F], w13[:, e * 4 * F:(e + 1) * 4 * F]).then_inc(S("w13_in"), 16)
            sp.wait_ge(S("rec_init_ready"), 2)
            sp.dma_start(rec_d.rearrange("(p t) c -> p (t c)", p=P), rec_init[:, :]).then_inc(S("rec_cleared"), 16)
        def project_sync(sp):
            def ld(dst_, src_):
                sp.dma_start(dst_, src_).then_inc(S("weights_in"), 16)
            rows = "(k p) n -> p k n"
            ld(wc[:, :, QK:QK + 2 * C], w_qkv[:, 0:2 * C].rearrange(rows, p=P))
            ld(wc[:, :, H0:H0 + C], w_hT.rearrange(rows, p=P))
            ld(wnat.rearrange("p (k n) -> p k n", k=2), w_h.rearrange(rows, p=P))
            ld(wa_sb.rearrange("p (k n) -> p k n", k=2), w_a.rearrange(rows, p=P))
            ld(wvt_sb.rearrange("p (k n) -> p k n", k=2), w_vT.rearrange(rows, p=P))
            ld(wout_sb.rearrange("p (k n) -> p k n", k=2), w_out.rearrange(rows, p=P))
            ld(bias[:, QK:QK + 2 * C], b_qkv[0:2 * C].unsqueeze(0).to_broadcast([P, 2 * C]))
            ld(bias[:, H0:H0 + C], b_h.unsqueeze(0).to_broadcast([P, C]))
            ld(bias[:, A0:A0 + 2], b_a.unsqueeze(0).to_broadcast([P, 2]))
            ld(bo_row[:, :], b_out.unsqueeze(0).to_broadcast([P, C]))
            ld(b_col[:, :], b_cols)

            def step(i, b):
                if not (isinstance(i, int) and i >= NT):
                    if due(i - 1):
                        sp.wait_ge(S("base_ready"), i - 1)
                    sp.dma_start(x_in[b][:, :], x.rearrange("(t p) c -> t p c", p=P)[i] if isinstance(i, int)
                                 else x.rearrange("(t p) c -> t p c", p=P)[bass.ds(i, 1), :, :].rearrange("a p c -> (a p) c"))\
                        .then_inc(S(f"x_in{b}"), 16)
                if not (isinstance(i, int) and i < 2):
                    j = i - 2
                    def tile_of(t):
                        return t[j] if isinstance(j, int) else t[bass.ds(j, 1), :, :].rearrange("a p c -> (a p) c")
                    if due(j + 1):
                        sp.wait_ge(S("table_ready"), j + 1)
                    sp.dma_start(tile_of(table_d[0:NT * P, :].rearrange("(t p) c -> t p c", p=P)), hb[b][:, :]).then_inc(S(f"row_out{b}"), 16)
                    if due(j + 1):
                        sp.wait_ge(S("base_ready"), j + 1)
                    sp.dma_start(tile_of(base_d), base[b][:, :]).then_inc(S(f"row_out{b}"), 16)
                    if due(j + 1):
                        sp.wait_ge(S("q2t_ready"), j + 1)
                    sp.sem_inc(S("sync_steps"), 1)
                    sp.dma_start(tile_of(q2t_d), q2t[b][:, :]).then_inc(S(f"row_out{b}"), 16)

            step(0, 0)
            step(1, 1)
            with sp.Fori(1, NT // 2) as k:
                step(k * 2, 0)
                step(k * 2 + 1, 1)
            step(NT, 0)
            step(NT + 1, 1)
            sp.wait_ge(S("zeros_ready"), 1)
            sp.dma_start(table_d[DUMMY:DUMMY + 1, :], zeros[0:1, 0:TW]).then_inc(S("cleared"), 16)
            sp.dma_start(out[NT * P:, :], zeros[:, 0:C]).then_inc(S("cleared"), 16)
            sp.dma_start(xs_d.rearrange("(p a r) c -> p a (r c)", p=P, r=2),
                         zeros.unsqueeze(1).to_broadcast([P, MT // 2, 2 * TW])).then_inc(S("cleared"), 16)
            sp.wait_ge(S("row_out0"), 48 * (NT // 2))
            sp.wait_ge(S("row_out1"), 48 * (NT // 2))
            sp.wait_ge(S("cleared"), 48)

        def project_tensor(pe):
            mm = nc.tensor.matmul
            pe.wait_ge(S("weights_in"), 16 * 11)
            wo = wout_sb.rearrange("p (k n) -> p k n", k=2)
            for c in range(2):
                for j in range(2):
                    mm(psum[1][:, c * C:(c + 1) * C], wvt_sb[:, j * C + c * P:j * C + c * P + P], wo[:, j, :],
                       start=(j == 0), stop=(j == 1))
            for c in range(2):
                for j in range(2):
                    mm(psum[2][:, 2 * c:2 * c + 2], wnat[:, j * C + c * P:j * C + c * P + P], wa_sb[:, 2 * j:2 * j + 2],
                       start=(j == 0), stop=(j == 1))
            for j in range(2):
                mm(psum[3][:, 0:C], b_col[:, j:j + 1].to_broadcast([P, P]), wo[:, j, :], start=(j == 0), stop=(j == 1))
            for j in range(2):
                last = mm(psum[4][:, 0:2], b_col[:, 2 + j:3 + j].to_broadcast([P, P]), wa_sb[:, 2 * j:2 * j + 2],
                          start=(j == 0), stop=(j == 1))
            last.then_inc(S("folded"), 1)
            pe.wait_ge(S("zeros_ready"), 1)
            mm(psum[5][:, :], ident[:, :], zeros[:, 0:512], start=True, stop=False, skip_group_check=True)
            mm(psum[6][:, :], ident[:, :], zeros[:, 0:512], start=True, stop=False, skip_group_check=True)
            pe.wait_ge(S("wcat_ready"), 1)

            def step(i, b):
                if not (isinstance(i, int) and i >= NT):
                    pe.wait_ge(S("xn_ready"), i + 1)
                    if due(i):
                        pe.wait_ge(S("xnt_ready"), i)
                    nc.tensor.transpose(psum[3][:, 0:P], xn[b][:, 0:P], ident[:, :])
                    nc.tensor.transpose(psum[3][:, P:C], xn[b][:, P:C], ident[:, :]).then_inc(S("xnt_done"), 1)
                    pe.wait_ge(S("xnt_ready"), i + 1)
                    if due(i - 1):
                        pe.wait_ge(S("qk_taken"), i - 1)
                    for c in range(2):
                        mm(psum[b][:, :], xnt[b][:, c * P:(c + 1) * P], wc[:, c, QK:QK + 2 * C], start=(c == 0), stop=(c == 1))\
                            .then_inc(S("qk_half"), 1)
                    if due(i):
                        pe.wait_ge(S("hv_taken"), i)
                    for c in range(2):
                        mm(psum[2][:, :], xnt[b][:, c * P:(c + 1) * P], wc[:, c, H0:H0 + 2 * C], start=(c == 0), stop=(c == 1))
                    for c in range(2):
                        last = mm(psum[7][:, 0:2], xnt[b][:, c * P:(c + 1) * P], wc[:, c, A0:A0 + 2], start=(c == 0), stop=(c == 1))
                    last.then_inc(S("hv_done"), 1)
                if not (isinstance(i, int) and i < 1):
                    j = i - 1
                    if due(j + 1):
                        pe.wait_ge(S("q2_ready"), j + 1)
                    if due(j):
                        pe.wait_ge(S("q2t_ready"), j)
                    nc.tensor.transpose(psum[4][:, 0:P], q2[:, 0:P], ident[:, :])
                    nc.tensor.transpose(psum[4][:, P:C], q2[:, P:C], ident[:, :]).then_inc(S("q2t_done"), 1)
                    if due(j + 1):
                        pe.wait_ge(S("kn_ready"), j + 1)
                    for c in range(2):
                        mm(psum[5][:, c * C:(c + 1) * C], xn[1 - b][:, c * P:(c + 1) * P], kn[:, :], start=False, stop=False,
                           skip_group_check=True)
                    mm(psum[6][0:1, 0:C], ones[:, 0:1], kn[:, :], start=False, stop=False, skip_group_check=True)
                    if due(j + 1):
                        pe.wait_ge(S("kn2_ready"), j + 1)
                    for c in range(2):
                        last = mm(psum[6][:, C + c:C + c + 1], kn2[:, c * P:(c + 1) * P], ones[:, 0:1], start=False, stop=False,
                                  skip_group_check=True)
                    last.then_inc(S("sums_done"), 1)

            step(0, 0)
            step(1, 1)
            with pe.Fori(1, NT // 2) as k:
                step(k * 2, 0)
                step(k * 2 + 1, 1)
            step(NT, 0)

        def sort_scalar(act):
            def count(i):
                act.wait_ge(S("hist_mask"), i * 2 + 2)
                nc.scalar.activation(mask[1][:, :], mask[1][:, :], ACT.Copy, accum_out=hist[:, ds(i * 2 + 1)])\
                    .then_inc(S("hist_acted"), 1)

            count(0)
            with act.Fori(1, NT // 2) as i:
                count(i)

        def project_scalar(act):
            a = nc.scalar.activation

            def step(i, b):
                if not (isinstance(i, int) and i >= NT):
                    act.wait_ge(S("var_ready"), i + 1)
                    a(rstd[:, 1:2], rstd[:, 0:1], ACT.Sqrt).then_inc(S("std_ready"), 1)
                    act.wait_ge(S("xnt_done"), i + 1)
                    a(xnt[b][:, :], psum[3][:, 0:C], ACT.Copy).then_inc(S("xnt_ready"), 1)
                if not (isinstance(i, int) and i < 1):
                    j = i - 1
                    if due(j + 1):
                        act.wait_ge(S("qk_taken"), j + 1)
                    if due(j):
                        act.wait_ge(S("kn_ready"), j)
                    a(k2[:, :], qk[:, C:2 * C], ACT.Square, accum_out=k2s[:, :]).then_inc(S("k2_ready"), 1)
                    if due(j):
                        act.wait_ge(S("q2t_done"), j)
                    if due(j):
                        act.wait_ge(S("q4_ready"), j)
                    col = slice(j, j + 1) if isinstance(j, int) else bass.ds(j, 1)
                    a(q2[:, :], qk[:, 0:C], ACT.Square, accum_out=q2s[:, col]).then_inc(S("q2_ready"), 1)
                    if due(j + 1):
                        act.wait_ge(S("q2_ready"), j + 1)
                    a(q4[:, :], q2[:, :], ACT.Square, accum_out=q4s[:, col]).then_inc(S("q4_ready"), 1)
                    if due(j + 1):
                        act.wait_ge(S("q2t_done"), j + 1)
                    if not (isinstance(j, int) and j < 2):
                        if due((j - (1 - b)) * 24):
                            act.wait_ge(S(f"row_out{1 - b}"), (j - (1 - b)) * 24)
                    a(q2t[1 - b][:, :], psum[4][:, 0:C], ACT.Copy).then_inc(S("q2t_ready"), 1)
                    if due(j + 1):
                        act.wait_ge(S("kn_ready"), j + 1)
                    if due(j):
                        act.wait_ge(S("sums_done"), j)
                    a(kn2[:, :], kn[:, :], ACT.Square).then_inc(S("kn2_ready"), 1)

            step(0, 0)
            step(1, 1)
            with act.Fori(1, NT // 2) as k:
                step(k * 2, 0)
                step(k * 2 + 1, 1)
            step(NT, 0)

        def project_vector(dve):
            v = nc.vector
            o = Order(dve, "v_fold")
            dve.wait_ge(S("folded"), 1)
            dve.wait_ge(S("pool_lanes"), 1)
            o(v.tensor_scalar(valid[:, :], lane_i[:, :], float(N), None, ALU.is_lt))
            for c in range(2):
                v.tensor_copy(wc[:, c, VO0:VO0 + C], psum[1][:, c * C:(c + 1) * C])
                v.tensor_copy(wc[:, c, A0:A0 + 2], psum[2][:, 2 * c:2 * c + 2])
            v.tensor_copy(bvo_row[:, :], psum[3][0:1, 0:C])
            v.tensor_tensor(bias[:, VO0:VO0 + C], psum[3][:, 0:C], bo_row[:, :], ALU.add)
            o(v.tensor_tensor(bias[:, A0:A0 + 2], psum[4][:, 0:2], bias[:, A0:A0 + 2], ALU.add))
            for c in range(2):
                v.tensor_reduce(mean_w[:, 2 * c:2 * c + 2], wc[:, c, 0:2 * C].rearrange("p (m n) -> p m n", m=2), AX.X, ALU.add)
            o(v.tensor_reduce(mean_w[:, 4:6], bias[:, 0:2 * C].rearrange("p (m n) -> p m n", m=2), AX.X, ALU.add))
            dve.wait_ge(S("v_fold"), o.n)
            o(v.tensor_scalar(mean_w[:, 0:6], mean_w[:, 0:6], 1.0 / C, None, ALU.mult))
            dve.wait_ge(S("v_fold"), o.n)
            for c in range(2):
                for m in range(2):
                    v.tensor_scalar(wc[:, c, m * C:(m + 1) * C], wc[:, c, m * C:(m + 1) * C],
                                    mean_w[:, 2 * c + m:2 * c + m + 1], None, ALU.subtract)
            for m in range(2):
                last = v.tensor_scalar(bias[:, m * C:(m + 1) * C], bias[:, m * C:(m + 1) * C], mean_w[:, 4 + m:5 + m], None,
                                       ALU.subtract)
            for b in range(2):
                last = v.memset(hb[b][:, C:C + 1], 1.0)
            last.then_inc(S("wcat_ready"), 1)
            dve.wait_ge(S("wcat_ready"), 1)

            def step(i, b):
                if not (isinstance(i, int) and i >= NT):
                    dve.wait_ge(S(f"x_in{b}"), (i - b) * 8 + 16)
                    v.bn_stats(st6[:, 0:6], x_in[b][:, :]).then_inc(S("ln_steps"), 1)
                    dve.wait_ge(S("ln_steps"), i * 3 + 1)
                    dve.sem_inc(S("vector_steps"), 1)
                    v.bn_aggr(mv[:, :], st6[:, 0:6]).then_inc(S("ln_steps"), 1)
                    dve.wait_ge(S("ln_steps"), i * 3 + 2)
                    v.tensor_scalar(rstd[:, 0:1], mv[:, 1:2], EPS, None, ALU.add).then_inc(S("var_ready"), 1)
                    dve.wait_ge(S("std_ready"), i + 1)
                    v.reciprocal(rstd[:, 0:1], rstd[:, 1:2]).then_inc(S("ln_steps"), 1)
                    dve.wait_ge(S("ln_steps"), i * 3 + 3)
                    if due(i - 1):
                        dve.wait_ge(S("sums_done"), i - 1)
                    v.tensor_scalar(xn[b][:, :], x_in[b][:, :], mv[:, 0:1], rstd[:, 0:1], ALU.subtract, ALU.mult)\
                        .then_inc(S("xn_ready"), 1)
                if not (isinstance(i, int) and i < 1):
                    j, bj = i - 1, 1 - b
                    if due(j * 2 + 2):
                        dve.wait_ge(S("qk_half"), j * 2 + 2)
                    if due(j):
                        dve.wait_ge(S("q2_ready"), j)
                    v.tensor_tensor(qk[:, :], psum[bj][:, :], bias[:, 0:2 * C], ALU.add).then_inc(S("qk_taken"), 1)
                    if due(j + 1):
                        dve.wait_ge(S("hv_done"), j + 1)
                    if not (isinstance(j, int) and j < 2):
                        if due((j - bj) * 24):
                            dve.wait_ge(S(f"row_out{bj}"), (j - bj) * 24)
                    v.tensor_tensor(hb[bj][:, 0:C], psum[2][:, 0:C], bias[:, H0:H0 + C], ALU.add)
                    v.tensor_tensor(hb[bj][:, C + 1:C + 2], psum[7][:, 1:2], bias[:, A0 + 1:A0 + 2], ALU.add)
                    cols = slice(2 * j, 2 * j + 2) if isinstance(j, int) else bass.ds(j * 2, 2)
                    v.tensor_tensor(a12[:, cols], psum[7][:, 0:2], bias[:, A0:A0 + 2], ALU.add).then_inc(S("table_ready"), 1)
                    v.tensor_tensor(base[bj][:, :], psum[2][:, C:2 * C], bias[:, VO0:VO0 + C], ALU.add).then_inc(S("hv_taken"), 1)
                    if due(j + 1):
                        dve.wait_ge(S("hv_taken"), j + 1)
                    v.tensor_tensor(base[bj][:, :], base[bj][:, :], x_in[bj][:, :], ALU.add).then_inc(S("base_ready"), 1)
                    if due(j + 1):
                        dve.wait_ge(S("k2_ready"), j + 1)
                    v.tensor_scalar(rk[:, :], k2s[:, :], 1e-7, None, ALU.add).then_inc(S("k_steps"), 1)
                    dve.wait_ge(S("k_steps"), j * 3 + 1)
                    v.reciprocal(rk[:, :], rk[:, :]).then_inc(S("k_steps"), 1)
                    dve.wait_ge(S("k_steps"), j * 3 + 2)
                    col = slice(j, j + 1) if isinstance(j, int) else bass.ds(j, 1)
                    v.tensor_tensor(rkv[:, :], rk[:, :], valid[:, col], ALU.mult).then_inc(S("k_steps"), 1)
                    dve.wait_ge(S("k_steps"), j * 3 + 3)
                    if due(j):
                        dve.wait_ge(S("sums_done"), j)
                    if due(j):
                        dve.wait_ge(S("kn2_ready"), j)
                    v.tensor_scalar(kn[:, :], k2[:, :], rkv[:, :], None, ALU.mult).then_inc(S("kn_ready"), 1)

            step(0, 0)
            step(1, 1)
            with dve.Fori(1, NT // 2) as k:
                step(k * 2, 0)
                step(k * 2 + 1, 1)
            step(NT, 0)

        def mix_scalar(act):
            act.wait_ge(S("gt_copied"), 1)
            nc.scalar.activation(kscale[:, :], psum[6][:, C:C + 2], ACT.Sqrt)
            act.wait_ge(S("q4_ready"), NT)
            nc.scalar.activation(fac2[:, :], q4s[:, :], ACT.Sqrt).then_inc(S("roots_ready"), 1)

        def mix_tensor(pe):
            mm = nc.tensor.matmul
            pe.wait_ge(S("gt_copied"), 1)
            for ck in range(2):
                for cx in range(2):
                    mm(psum[1][:, ck * C:(ck + 1) * C], gt_sb[:, cx * C + ck * P:cx * C + ck * P + P], wc[:, cx, VO0:VO0 + C],
                       start=(cx == 0), stop=False)
                last = mm(psum[1][:, ck * C:(ck + 1) * C], g1_row[:, ck * P:(ck + 1) * P], bvo_row[:, :], start=False, stop=True)
            last.then_inc(S("kw_done"), 1)
        def mix_vector(dve):
            v = nc.vector
            o = Order(dve, "v_mix")
            dve.wait_ge(S("sums_done"), NT)
            v.tensor_copy(gt_sb[:, :], psum[5][:, :])
            v.tensor_copy(g1_row[:, :], psum[6][0:1, 0:C]).then_inc(S("gt_copied"), 1)
            dve.wait_ge(S("roots_ready"), 1)
            o(v.tensor_scalar(kscale[:, :], kscale[:, :], 1e-12, None, ALU.max))
            dve.wait_ge(S("v_mix"), o.n)
            o(v.reciprocal(kscale[:, :], kscale[:, :]))
            dve.wait_ge(S("q4_ready"), NT)
            o(v.tensor_scalar(fac[:, :], q2s[:, :], 1e-7, None, ALU.add))
            dve.wait_ge(S("v_mix"), o.n)
            o(v.reciprocal(fac[:, :], fac[:, :]))
            dve.wait_ge(S("v_mix"), o.n)
            o(v.tensor_tensor(fac2[:, :], fac2[:, :], fac[:, :], ALU.mult))
            dve.wait_ge(S("v_mix"), o.n)
            o(v.tensor_scalar(fac2[:, :], fac2[:, :], 1e-12, None, ALU.max))
            dve.wait_ge(S("v_mix"), o.n)
            o(v.reciprocal(fac2[:, :], fac2[:, :]))
            dve.wait_ge(S("v_mix"), o.n)
            o(v.tensor_tensor(fac[:, :], fac[:, :], fac2[:, :], ALU.mult))
            dve.wait_ge(S("kw_done"), 1)
            for ck in range(2):
                last = v.tensor_scalar(kw_sb[:, ck * C:(ck + 1) * C], psum[1][:, ck * C:(ck + 1) * C], kscale[:, ck:ck + 1],
                                       float(N) ** -0.5, ALU.mult, ALU.mult)
            last.then_inc(S("kw_ready"), 1)

        def tables_tensor(pe):
            mm = nc.tensor.matmul
            H = GT // 2
            pe.wait_ge(S("kw_ready"), 1)
            nc.tensor.transpose(psum[0][0:NT, 0:P], first[:, 0:NT], ident[:, :])
            nc.tensor.transpose(psum[0][0:NT, P:2 * P], first[:, NT:2 * NT], ident[:, :])
            nc.tensor.transpose(psum[0][0:NT, 2 * P:3 * P], a12.rearrange("p (t c) -> p t c", c=2)[:, :, 0], ident[:, :])\
                .then_inc(S("turned"), 1)
            pe.wait_ge(S("a2_least"), 1)
            nc.tensor.transpose(psum[7][0:1, 0:P], small[:, 0:1], ident[:, :]).then_inc(S("least_turned"), 1)
            pe.wait_ge(S("tables_ready"), 1)
            for h in range(2):
                mm(psum[1 + h][:, 0:H], ones[0:NT, :], prod[0:NT, h * H:(h + 1) * H], start=True, stop=True)
                mm(psum[3 + h][:, 0:H], a1_rows[0:NT, :], ohb[0:NT, h * H:(h + 1) * H], start=True, stop=True)
                mm(psum[5 + h][0:1, 0:H], bweight[0:NT, :], ohb[0:NT, h * H:(h + 1) * H], start=True, stop=True)
            mm(psum[0][:, 0:1], ones[0:1, :], small[0:1, 2:3], start=True, stop=True).then_inc(S("tables_done"), 1)

        def tables_vector(dve):
            v = nc.vector
            o = Order(dve, "v_tables")
            H = GT // 2
            o(v.tensor_copy(tile_f[:, :], tile_i[:, :]))
            o(v.tensor_scalar(bweight[:, :], lane_i[:, 0:1], -1.0, float(NT - 1), ALU.mult, ALU.add))
            v.tensor_reduce(small[:, 0:1], a12.rearrange("p (t c) -> p t c", c=2)[:, :, 1], AX.X, ALU.min)\
                .then_inc(S("a2_least"), 1)
            dve.wait_ge(S("turned"), 1)
            v.tensor_copy(edge[0:NT, 0:1], psum[0][0:NT, 0:1])
            v.tensor_copy(edge[0:NT, 1:2], psum[0][0:NT, P:P + 1])
            o(v.tensor_copy(a1_rows[0:NT, :], psum[0][0:NT, 2 * P:3 * P]))
            dve.wait_ge(S("v_tables"), o.n)
            o(v.tensor_scalar(prod[0:NT, :], tile_f[0:NT, :], edge[0:NT, 1:2], None, ALU.is_lt))
            dve.wait_ge(S("v_tables"), o.n)
            o(v.scalar_tensor_tensor(ohb[0:NT, :], tile_f[0:NT, :], edge[0:NT, 0:1], prod[0:NT, :], ALU.is_ge, ALU.mult))
            dve.wait_ge(S("least_turned"), 1)
            o(v.tensor_reduce(small[0:1, 1:2], psum[7][0:1, 0:P], AX.X, ALU.min))
            dve.wait_ge(S("v_tables"), o.n)
            v.memset(prod[0:NT, 0:1], 0.0)
            v.tensor_tensor(prod[0:NT, 1:GT], ohb[0:NT, 1:GT], ohb[0:NT, 0:GT - 1], ALU.mult)
            v.tensor_scalar(small[0:1, 2:3], small[0:1, 1:2], -1.0, 1.0, ALU.mult, ALU.add).then_inc(S("tables_ready"), 1)
            dve.wait_ge(S("tables_done"), 1)
            for h in range(2):
                v.tensor_copy(same[:, h * H:(h + 1) * H], psum[1 + h][:, 0:H])
                v.tensor_copy(a1t[:, h * H:(h + 1) * H], psum[3 + h][:, 0:H])
                v.tensor_scalar(bt_i[0:1, h * H:(h + 1) * H], psum[5 + h][0:1, 0:H], -float(TW), float((NT - 1) * TW),
                                ALU.mult, ALU.add)
            v.tensor_copy(shift[:, :], psum[0][:, 0:1])

        def steady(eng, step, lag):
            for i in range(RING):
                step(i, i, 0)
            with eng.Fori(1, NG // RING) as k:
                for j in range(RING):
                    step(k * RING + j, j, k)
            for i in range(NG // RING * RING, NG + lag):
                step(i, i % RING, i // RING)

        def live(i, lag, n=NG):
            return not isinstance(i, int) or 0 <= i - lag < n

        def gather_pool(pool):
            pool.wait_ge(S("records_in"), 16)

            def step(i, j, k):
                if live(i, 0):
                    if due((i - RING + 1) * G):
                        pool.wait_ge(S("product_done"), (i - RING + 1) * G)
                    pool.tensor_copy(idx_g[j][:, :], rec_all.rearrange("p (t c) -> p t c", c=2)[:, ds(i * G, G), 1])\
                        .then_inc(S("indices_ready"), 1)
                    pool.wait_ge(S("indices_ready"), i + 1)
                    pool.sem_inc(S("pool_steps"), 1)
                    for q in range(G):
                        pool.indirect_dma_start(rows_in[j][:, q * TW:(q + 1) * TW], None, table_d[:, :],
                                                bass.IndirectOffsetOnAxis(ap=idx_g[j][:, q:q + 1], axis=0))\
                            .then_inc(S(f"rows_in{j}"), 16)

            steady(pool, step, 0)

        def gather_tensor(pe):
            mm = nc.tensor.matmul

            def step(i, j, k):
                if live(i, 2):
                    b, t = j % 2, i - 2
                    pe.wait_ge(S("shift_ready"), t + 1)
                    pe.wait_ge(S("member_ready"), t + 1)
                    if due(t - 1):
                        pe.wait_ge(S("z_ready"), t - 1)
                    for q in range(G):
                        last = mm(psum[2 + b][:, 2 * q:2 * q + 2], member[b][:, q * P:(q + 1) * P], lb[b][:, q:q + G + 2:G + 1],
                                  start=True, stop=True)
                    last.then_inc(S("edge_done"), 1)
                if live(i, 4):
                    b, g, t = j % 2, (j - 4) % RING, i - 4
                    for q in range(G):
                        pe.wait_ge(S("weight_ready"), t * G + q + 1)
                        if due((t - 1) * G + q + 1):
                            pe.wait_ge(S("acc_done"), (t - 1) * G + q + 1)
                        mm(psum[4 + q][:, 0:C + 1], weight[b][:, q * P:(q + 1) * P], rows_in[g][:, q * TW:q * TW + C + 1],
                           start=True, stop=True).then_inc(S("product_done"), 1)
                if live(i, 0):
                    b = j % 2
                    if due(i - 1):
                        pe.wait_ge(S("member_ready"), i - 1)
                    for q in range(G):
                        pe.wait_ge(S("masked_ready"), i * G + q + 1)
                        last = nc.tensor.transpose(psum[b][:, q * P:(q + 1) * P], masked[b][:, q * P:(q + 1) * P], ident[:, :])
                    last.then_inc(S("masked_turned"), 1)

            steady(pe, step, 4)

        def gather_scalar(act):
            a = nc.scalar.activation

            def step(i, j, k):
                if live(i, 0):
                    act.wait_ge(S("hot_ready"), i + 1)
                    if due(i - 1):
                        act.wait_ge(S("masked_turned"), i - 1)
                    for q in range(G):
                        a(masked[j % 2][:, q * P:(q + 1) * P], hot[j][:, q * P:(q + 1) * P], ACT.Copy,
                          scale=a2s[j % 2][:, q:q + 1]).then_inc(S("masked_ready"), 1)
                if live(i, 3):
                    b, t = (j - 3) % 2, i - 3
                    act.wait_ge(S("z_ready"), t + 1)
                    if due((t - 1) * G):
                        act.wait_ge(S("weight_ready"), (t - 1) * G)
                    a(wexp[b][:, :], zarg[:, :], ACT.Exp).then_inc(S("wexp_ready"), 1)
                    act.wait_ge(S("wexp_ready"), t + 1)
                    if due((t - 1) * G):
                        act.wait_ge(S("product_done"), (t - 1) * G)
                    for q in range(G):
                        a(weight[b][:, q * P:(q + 1) * P], hot[(j - 3) % RING][:, q * P:(q + 1) * P], ACT.Copy,
                          scale=wexp[b][:, q:q + 1]).then_inc(S("weight_ready"), 1)
                if live(i, 1):
                    b = (j - 1) % 2
                    act.wait_ge(S("max_done"), i)
                    if due(i - 2):
                        act.wait_ge(S("edge_done"), i - 2)
                    a(member[b][:, :], psum[b][:, :], ACT.Sign).then_inc(S("member_ready"), 1)
                    act.wait_ge(S("dm_ready"), i)
                    if due((i - RING) * G):
                        act.wait_ge(S("acc_done"), (i - RING) * G)
                    a(alpha[(j - 1) % RING][:, :], dm[:, :], ACT.Exp).then_inc(S("alpha_ready"), 1)

            steady(act, step, 3)

        def gather_vector(dve):
            v = nc.vector
            v.memset(nb[1][:, :], 0.0)
            v.memset(lb[1][:, :], 0.0)
            v.memset(acc[:, :], 0.0).then_inc(S("acc_cleared"), 1)
            dve.wait_ge(S("records_in"), 16)
            ra = rec_all.rearrange("p (t c) -> p t c", c=2)
            v.tensor_copy(iota_b[:, :], iota[:, :])
            v.tensor_copy(lane_row[:, :], ra[:, :, 0]).then_inc(S("acc_cleared"), 1)
            dve.wait_ge(S("acc_cleared"), 2)

            def exponents(i, j, part):
                if not live(i, 3):
                    return
                b, t = (j - 3) % 2, i - 3
                pm = psum[2 + b][:, 0:2 * G].rearrange("p (q c) -> p q c", c=2)
                if part == 0:
                    gv = rows_in[(j - 3) % RING].rearrange("p (q c) -> p q c", c=TW)
                    dve.wait_ge(S("edge_done"), t + 1)
                    if due(t):
                        dve.wait_ge(S("wexp_ready"), t)
                    v.tensor_tensor(score[:, :], pm[:, :, 0], gv[:, :, C + 1], ALU.add).then_inc(S("z_steps"), 1)
                elif part == 1:
                    dve.wait_ge(S("z_steps"), t * 2 + 1)
                    v.scalar_tensor_tensor(leaky[:, :], score[:, :], SLOPE, score[:, :], ALU.mult, ALU.max).then_inc(S("z_steps"), 1)
                else:
                    dve.wait_ge(S("z_steps"), t * 2 + 2)
                    v.tensor_tensor(zarg[:, :], leaky[:, :], pm[:, :, 1], ALU.subtract).then_inc(S("z_ready"), 1)

            def add(i, j, q, columns):
                if not live(i, 5):
                    return
                t = i - 5
                if q == 0:
                    dve.wait_ge(S("alpha_ready"), t + 1)
                dve.wait_ge(S("product_done"), t * G + q + 1)
                if due(t * G + q):
                    dve.wait_ge(S("acc_done"), t * G + q)
                here = acc[:, bass.ds(columns[q], C + 1)]
                v.scalar_tensor_tensor(here, here, alpha[(j - 5) % RING][:, q:q + 1], psum[4 + q][:, 0:C + 1],
                                       ALU.mult, ALU.add).then_inc(S("acc_done"), 1)

            def step(i, j, k):
                columns = None
                if live(i, 0):
                    b = j % 2
                    dve.wait_ge(S(f"rows_in{j}"), k * (16 * G) + 16 * G)
                    if due((i - 1) * G):
                        dve.wait_ge(S("masked_ready"), (i - 1) * G)
                    gv = rows_in[j].rearrange("p (q c) -> p q c", c=TW)
                    v.tensor_scalar(a2s[b][:, :], gv[:, :, C + 1], shift[:, :], 0.5, ALU.add, ALU.max)
                    if due((i - RING + 1) * G):
                        dve.wait_ge(S("weight_ready"), (i - RING + 1) * G)
                    v.tensor_tensor(hot[j].rearrange("p (q r) -> p q r", q=G),
                                    iota_b.unsqueeze(1).to_broadcast([P, G, P]),
                                    lane_row[:, ds(i * G, G)].unsqueeze(2).to_broadcast([P, G, P]), ALU.is_equal)\
                        .then_inc(S("hot_ready"), 1)
                if live(i, 5):
                    _, columns = nc.values_load_multi_w_load_instructions(
                        bt_i[0:1, ds((i - 5) * G, G)], engines=(dve.engine,), min_val=0, max_val=(NT - 1) * TW,
                        skip_runtime_bounds_check_because="the table holds first columns of buckets")
                add(i, j, 0, columns)
                exponents(i, j, 0)
                if live(i, 1):
                    b, t = (j - 1) % 2, i - 1
                    if due(t - 1):
                        dve.wait_ge(S("edge_done"), t - 1)
                    v.tensor_copy(lb[b][:, 0:G], a1t[:, ds(t * G, G)])
                add(i, j, 1, columns)
                exponents(i, j, 1)
                if live(i, 1):
                    dve.wait_ge(S("masked_turned"), t + 1)
                    if due(t):
                        dve.wait_ge(S("nb_steps"), t)
                    v.tensor_reduce(tile_max[:, :], psum[b].rearrange("p (q r) -> p q r", q=G)[:, :, :], AX.X, ALU.max)\
                        .then_inc(S("max_done"), 1)
                exponents(i, j, 2)
                add(i, j, 2, columns)
                if live(i, 1):
                    dve.wait_ge(S("max_done"), t + 1)
                    if due(t):
                        dve.wait_ge(S("lin_steps"), t)
                    v.tensor_tensor_scan(nb[b][:, :], same[:, ds(t * G, G)], tile_max[:, :], nb[1 - b][:, G - 1:G],
                                         ALU.mult, ALU.max).then_inc(S("nb_steps"), 1)
                    if due(t):
                        dve.wait_ge(S("shift_ready"), t)
                    if due(t - 1):
                        dve.wait_ge(S("dm_steps"), t - 1)
                    v.tensor_copy(lb[b][:, G:G + 1], lb[1 - b][:, 2 * G:2 * G + 1])
                    dve.wait_ge(S("nb_steps"), t + 1)
                    v.scalar_tensor_tensor(lin[:, :], nb[b][:, :], shift[:, :], a1t[:, ds(t * G, G)],
                                           ALU.subtract, ALU.add).then_inc(S("lin_steps"), 1)
                add(i, j, 3, columns)
                if live(i, 1):
                    dve.wait_ge(S("lin_steps"), t + 1)
                    v.scalar_tensor_tensor(lb[b][:, G + 1:2 * G + 1], lin[:, :], SLOPE, lin[:, :], ALU.mult, ALU.max)\
                        .then_inc(S("shift_ready"), 1)
                    dve.wait_ge(S("shift_ready"), t + 1)
                    if due(t):
                        dve.wait_ge(S("dm_ready"), t)
                    v.tensor_tensor(dm0[:, :], lb[b][:, G:2 * G], lb[b][:, G + 1:2 * G + 1], ALU.subtract)\
                        .then_inc(S("dm_steps"), 1)
                    dve.wait_ge(S("dm_steps"), t + 1)
                    if due(t):
                        dve.wait_ge(S("alpha_ready"), t)
                    v.tensor_tensor(dm[:, :], dm0[:, :], same[:, ds(t * G, G)], ALU.mult).then_inc(S("dm_ready"), 1)

            steady(dve, step, 5)

        def pairs(eng, step, lag, n=NT):
            step(0, 0)
            step(1, 1)
            with eng.Fori(1, n // 2) as k:
                step(k * 2, 0)
                step(k * 2 + 1, 1)
            for i in range(n, n + lag):
                step(i, i % 2)

        def quads(eng, step, lag):
            for i in range(8):
                step(i, i % 4, i // 4)
            with eng.Fori(2, NT // 4) as k:
                for j in range(4):
                    step(k * 4 + j, j, k)
            for i in range(NT // 4 * 4, NT + lag):
                step(i, i % 4, i // 4)

        def route_sync(sp):
            sp.dma_start(router.rearrange("p (k n) -> p k n", k=2), w_router.rearrange("(k p) n -> p k n", p=P))\
                .then_inc(S("router_in"), 16)

            def step(i, j, k):
                if live(i, 0, NT):
                    if due(i - 3):
                        sp.wait_ge(S("x2_ready"), after("x2_ready", i - 3))
                    sp.dma_start(mix_in[j][:, :], tile_of(mix_d, i)).then_inc(S(f"mix_in{j}"), 16)
                if live(i, 3, NT):
                    sp.wait_ge(S("x2_ready"), after("x2_ready", i - 2))
                    sp.dma_start(tile_of(out[0:NT * P, :].rearrange("(t p) c -> t p c", p=P), i - 3), acc[:, ds((i - 3) * TW, C)]).then_inc(S("x2_out"), 16)
                if live(i, 5, NT):
                    place = (j - 5) % 4
                    sp.wait_ge(S("xn2_ready"), after("xn2_ready", i - 4))
                    sp.dma_start(tile_of(xn2_d, i - 5), xn2[place][:, :]).then_inc(S(f"xn2_out{place}"), 16)

            quads(sp, step, 5)
            sp.wait_ge(S("x2_out"), 16 * NT)
            for j in range(4):
                sp.wait_ge(S(f"xn2_out{j}"), after(f"xn2_out{j}", 16 * len(range(j, NT, 4))))

        def route_tensor(pe):
            mm = nc.tensor.matmul
            pe.wait_ge(S("router_in"), 16)

            def step(i, j, k):
                b = j % 2
                if live(i, 0, NT):
                    pe.wait_ge(S(f"mix_in{j}"), after(f"mix_in{j}", k * 16 + 16))
                    if due(i - 1):
                        pe.wait_ge(S("half_ready"), i - 1)
                    for c in range(2):
                        last = mm(psum[b][:, 0:C], mix_q[j][:, c * P:(c + 1) * P], kw_sb[:, c * C:(c + 1) * C],
                                  start=(c == 0), stop=(c == 1))
                    last.then_inc(S("mix_done"), 1)
                if live(i, 5, NT):
                    bl, t = (j - 5) % 2, i - 5
                    pe.wait_ge(S("xn2t_ready"), after("xn2t_ready", t + 1))
                    if due(t - 1):
                        pe.wait_ge(S("logits_ready"), after("logits_ready", t - 1))
                    for c in range(2):
                        last = mm(psum[4 + bl][:, 0:NE], xn2t[bl][:, c * P:(c + 1) * P], router[:, c * NE:(c + 1) * NE],
                                  start=(c == 0), stop=(c == 1))
                    last.then_inc(S("logits_done"), 1)
                if live(i, 4, NT):
                    bt, t = (j - 4) % 2, i - 4
                    pe.wait_ge(S("xn2_ready"), after("xn2_ready", t + 1))
                    if due(t - 1):
                        pe.wait_ge(S("xn2t_ready"), after("xn2t_ready", t - 1))
                    nc.tensor.transpose(psum[2 + bt][:, 0:P], xn2[(j - 4) % 4][:, 0:P], ident[:, :])
                    nc.tensor.transpose(psum[2 + bt][:, P:C], xn2[(j - 4) % 4][:, P:C], ident[:, :]).then_inc(S("xn2_turned"), 1)

            quads(pe, step, 5)
            pe.wait_ge(S("totals_ready"), 1)
            mm(psum[6][:, 0:NE], ones[:, :], tot[:, :], start=True, stop=True)
            mm(psum[6][:, NE:2 * NE], before[:, :], tot[:, :], start=True, stop=True).then_inc(S("totals_done"), 1)

        def route_scalar(act):
            def step(i, j, k):
                b = j % 2
                if live(i, 2, NT):
                    t = i - 2
                    act.wait_ge(S("var2_ready"), t + 1)
                    nc.scalar.activation(std2[b][:, 1:2], std2[b][:, 0:1], ACT.Sqrt).then_inc(S("std2_ready"), 1)
                if live(i, 4, NT):
                    bt, t = (j - 4) % 2, i - 4
                    act.wait_ge(S("xn2_turned"), t + 1)
                    if due(t - 1):
                        act.wait_ge(S("logits_done"), after("logits_done", t - 1))
                    nc.scalar.activation(xn2t[bt][:, :], psum[2 + bt][:, 0:C], ACT.Copy).then_inc(S("xn2t_ready"), 1)

            quads(act, step, 4)
            act.wait_ge(S("exponents_ready"), 1)
            nc.scalar.activation(scr[:, 0:NT * NE], scr[:, 0:NT * NE], ACT.Exp)
            nc.scalar.activation(pz[:, 0:NT], pz[:, 0:NT], ACT.Exp).then_inc(S("exps_ready"), 1)

        def route_vector(dve):
            v = nc.vector
            o = Order(dve, "v_route")
            den = acc.rearrange("p (t c) -> p t c", c=TW)[:, :, C]
            o(v.tensor_scalar(rden[:, :], den, 1e-30, None, ALU.max))
            dve.wait_ge(S("v_route"), o.n)
            o(v.reciprocal(rden[:, :], rden[:, :]))
            dve.wait_ge(S("v_route"), o.n)

            def step(i, j, k):
                b = j % 2
                if live(i, 2, NT):
                    t = i - 2
                    dve.wait_ge(S("x2_ready"), after("x2_ready", t + 1))
                    if due(t):
                        dve.wait_ge(S("mv_done"), t)
                    dve.sem_inc(S("vector_steps"), 1)
                    v.bn_stats(st2[:, :], acc[:, ds(t * TW, C)]).then_inc(S("st_done"), 1)
                if live(i, 0, NT):
                    dve.wait_ge(S("mix_done"), i + 1)
                    dve.wait_ge(S(f"mix_in{j}"), after(f"mix_in{j}", k * 16 + 16))
                    v.scalar_tensor_tensor(mix_b[j][:, :], psum[b][:, 0:C], fac[:, ds(i)], mix_b[j][:, :], ALU.mult, ALU.add)\
                        .then_inc(S("half_ready"), 1)
                if live(i, 2, NT):
                    dve.wait_ge(S("st_done"), t + 1)
                    if due(t - 1):
                        dve.wait_ge(S("xn2_ready"), after("xn2_ready", t - 1))
                    dve.sem_inc(S("vector_steps"), 1)
                    v.bn_aggr(mv2[b][:, :], st2[:, :]).then_inc(S("mv_done"), 1)
                if live(i, 1, NT):
                    t1 = i - 1
                    here = acc[:, ds(t1 * TW, C)]
                    dve.wait_ge(S("half_ready"), t1 + 1)
                    v.scalar_tensor_tensor(here, here, rden[:, ds(t1)], mix_b[(j - 1) % 4][:, :], ALU.mult, ALU.add)\
                        .then_inc(S("x2_ready"), 1)
                if live(i, 2, NT):
                    dve.wait_ge(S("mv_done"), t + 1)
                    v.tensor_scalar(std2[b][:, 0:1], mv2[b][:, 1:2], EPS, None, ALU.add).then_inc(S("var2_ready"), 1)
                if live(i, 3, NT):
                    bt, t3 = (j - 3) % 2, i - 3
                    dve.wait_ge(S("std2_ready"), t3 + 1)
                    v.reciprocal(std2[bt][:, 0:1], std2[bt][:, 1:2]).then_inc(S("rstd2_ready"), 1)
                if live(i, 6, NT):
                    bl, tl = (j - 6) % 2, i - 6
                    dve.wait_ge(S("logits_done"), after("logits_done", tl + 1))
                    v.tensor_copy(logits[:, ds(tl * NE, NE)], psum[4 + bl][:, 0:NE]).then_inc(S("logits_ready"), 1)
                if live(i, 3, NT):
                    dve.wait_ge(S("rstd2_ready"), t3 + 1)
                    if due(t3 - 3):
                        dve.wait_ge(S("xn2_turned"), t3 - 3)
                    place = (j - 3) % 4
                    turn = t3 // 4 if isinstance(i, int) else (k if j == 3 else k - 1)
                    if not isinstance(i, int) or turn > 0:
                        dve.wait_ge(S(f"xn2_out{place}"), after(f"xn2_out{place}", turn * 16))
                    v.tensor_scalar(xn2[(j - 3) % 4][:, :], acc[:, ds(t3 * TW, C)], mv2[bt][:, 0:1], std2[bt][:, 0:1],
                                    ALU.subtract, ALU.mult).then_inc(S("xn2_ready"), 1)

            quads(dve, step, 6)
            dve.wait_ge(S("logits_ready"), after("logits_ready", NT))
            dve.wait_ge(S("xn2_ready"), after("xn2_ready", NT))
            dve.wait_ge(S("x2_out"), 16 * NT)

            def step(ins):
                o(ins)
                dve.wait_ge(S("v_route"), o.n)
            L3 = logits.rearrange("p (t e) -> p t e", e=NE)
            O1 = oh12[:, 0:NT * NE].rearrange("p (t e) -> p t e", e=NE)
            O2 = oh12[:, NT * NE:2 * NT * NE].rearrange("p (t e) -> p t e", e=NE)
            S3 = scr[:, 0:NT * NE].rearrange("p (t e) -> p t e", e=NE)
            S4 = scr[:, NT * NE:2 * NT * NE].rearrange("p (t e) -> p t e", e=NE)
            nb3 = nidx.unsqueeze(1).to_broadcast([P, NT, NE])

            def bc(ap):
                return ap.unsqueeze(2).to_broadcast([P, NT, NE])
            step(v.tensor_scalar(nidx[:, :], iota[:, 0:NE], -1.0, float(NE), ALU.mult, ALU.add))
            for k, (src_, hot) in enumerate(((L3, O1), (S4, O2))):
                tk = top[:, k * NT:(k + 1) * NT]
                step(v.tensor_reduce(tk, src_, AX.X, ALU.max))
                step(v.tensor_tensor(S3, src_, bc(tk), ALU.is_equal))
                step(v.tensor_tensor(S3, S3, nb3, ALU.mult))
                step(v.tensor_reduce(ti[:, :], S3, AX.X, ALU.max))
                step(v.tensor_tensor(hot, nb3, bc(ti[:, :]), ALU.is_equal))
                if k == 0:
                    step(v.scalar_tensor_tensor(scr[:, NT * NE:2 * NT * NE], oh12[:, 0:NT * NE], -3e38, logits[:, :],
                                                ALU.mult, ALU.add))
            o(v.tensor_tensor(S3, L3, bc(top[:, 0:NT]), ALU.subtract))
            v.tensor_tensor(pz[:, 0:NT], top[:, NT:2 * NT], top[:, 0:NT], ALU.subtract).then_inc(S("exponents_ready"), 1)
            dve.wait_ge(S("exps_ready"), 1)
            step(v.tensor_reduce(pz[:, NT:2 * NT], S3, AX.X, ALU.add))
            step(v.reciprocal(pz[:, NT:2 * NT], pz[:, NT:2 * NT]))
            step(v.tensor_tensor(pz[:, 2 * NT:3 * NT], pz[:, 0:NT], pz[:, NT:2 * NT], ALU.mult))
            step(v.scalar_tensor_tensor(pz[:, 3 * NT:4 * NT], pz[:, NT:2 * NT], 1e-9, pz[:, 2 * NT:3 * NT], ALU.add, ALU.add))
            step(v.reciprocal(pz[:, 3 * NT:4 * NT], pz[:, 3 * NT:4 * NT]))
            step(v.tensor_tensor(gate[:, 0:NT], pz[:, NT:2 * NT], pz[:, 3 * NT:4 * NT], ALU.mult))
            step(v.tensor_tensor(gate[:, NT:2 * NT], pz[:, 2 * NT:3 * NT], pz[:, 3 * NT:4 * NT], ALU.mult))
            for hot in (O1, O2):
                step(v.tensor_tensor(hot, hot, bc(valid[:, :]), ALU.mult))
            incl = pre_a
            for e in range(NE):
                last = v.tensor_tensor_scan(incl.rearrange("p (t e) -> p t e", e=NE)[:, :, e], ones[:, 0:2 * NT],
                                            oh12.rearrange("p (t e) -> p t e", e=NE)[:, :, e], 0.0, ALU.mult, ALU.add)
            step(last)
            v.tensor_copy(tot[:, :], incl[:, (2 * NT - 1) * NE:2 * NT * NE]).then_inc(S("totals_ready"), 1)
            step(v.tensor_tensor(scr[:, :], incl[:, :], oh12[:, :], ALU.subtract))
            dve.wait_ge(S("totals_done"), 1)
            step(v.tensor_scalar(etile_i[:, :], psum[6][:, 0:NE], float(P - 1), None, ALU.add))
            step(v.tensor_scalar(etile_i[:, :], etile_i[:, :], 7, None, ALU.logical_shift_right))
            step(v.memset(escan[:, :], 0.0))
            W = 2 * NE
            step(v.tensor_copy(escan[:, NE:W], etile_i[:, :]))
            cur = 0
            for d in (1, 2, 4):
                a_, b_ = cur * W, (1 - cur) * W
                step(v.tensor_tensor(escan[:, b_ + NE:b_ + W], escan[:, a_ + NE:a_ + W], escan[:, a_ + NE - d:a_ + W - d], ALU.add))
                cur = 1 - cur
            step(v.tensor_copy(eend[:, :], escan[:, cur * W + NE:cur * W + W]))
            step(v.tensor_tensor(efirst[:, :], eend[:, :], etile_i[:, :], ALU.subtract))
            step(v.scalar_tensor_tensor(ebase[:, :], efirst[:, :], float(P), psum[6][:, NE:2 * NE], ALU.mult, ALU.add))
            R3v = scr.rearrange("p (t e) -> p t e", e=NE)
            step(v.tensor_tensor(R3v, R3v, ebase.unsqueeze(1).to_broadcast([P, 2 * NT, NE]), ALU.add))
            step(v.tensor_tensor(scr[:, :], scr[:, :], oh12[:, :], ALU.mult))
            step(v.tensor_reduce(pos_f[:, :], R3v, AX.X, ALU.add))
            step(v.tensor_copy(pos_i[:, :], pos_f[:, :]))
            fv = fields.rearrange("p (k t c) -> p k t c", k=2, c=2)
            for k in range(2):
                v.tensor_copy(fv[:, k, :, 0], token_i[:, :])
                step(v.tensor_copy(fv[:, k, :, 1], gate[:, k * NT:(k + 1) * NT]))
            step(v.tensor_copy(spare[:, :], spare_i[:, :]))
            T3 = tcmp.rearrange("p (t e) -> p t e", e=NE)
            step(v.tensor_tensor(T3, iota.unsqueeze(2).to_broadcast([P, P, NE]), eend.unsqueeze(1).to_broadcast([P, P, NE]), ALU.is_ge))
            step(v.tensor_reduce(ecount[:, :], T3, AX.X, ALU.add))
            step(v.tensor_scalar(et_i[:, :], ecount[:, :], float(NE - 1), None, ALU.min))

        NFULL = N // P

        def fours(eng, step, lag):
            for i in range(4):
                step(i, i)
            with eng.Fori(1, NFULL // 4) as k:
                for j in range(4):
                    step(k * 4 + j, j)
            for i in range(NFULL, NFULL + 1 + lag):
                step(i, i % 4)

        def lanes(i):
            return LAST_LANES if isinstance(i, int) and i == NFULL else P

        LAST_LANES = N - NFULL * P

        def dispatch_sync(sp):
            piece = NE * FC * C // (NFULL // 4)

            def step(i, j):
                if not (isinstance(i, int) and i < 4):
                    if due((i - j) * 8):
                        sp.wait_ge(S(f"sent{j}"), (i - j) * 8)
                for k in range(2):
                    sp.dma_start(xd[j][k][:, 0:C], tile_of(xn2_d, i)).then_inc(S(f"xd_in{j}"), 16)
                if j == 1 and not (isinstance(i, int) and i < 4):
                    late = LATE * 4 * F // (NFULL // 4 - 1)
                    part = ds((i - 5) * (late // 4) + (NE - LATE) * 4 * F, late)
                    sp.dma_start(w13_sb[:, part], w13[:, part]).then_inc(S("w13_in"), 16)
                if j == 3:
                    part = ds((i - 3) * (piece // 4), piece)
                    sp.dma_start(w2_sb[:, part], w2[:, part]).then_inc(S("w2_in"), 16)

            fours(sp, step, 0)

        def slots_of(pool, i, j):
            pool.tensor_copy(idx_d[j][:, :], pos_i.rearrange("p (k t) -> p t k", k=2)[:, ds(i), :].rearrange("p a k -> p (a k)"))\
                .then_inc(S("slots_copied"), 1)

        def dispatch_vector(dve):
            fv = fields.rearrange("p (k t c) -> p k t c", k=2, c=2)

            def step(i, j):
                if not (isinstance(i, int) and i < 4):
                    if due((i - j) * 8):
                        dve.wait_ge(S(f"sent{j}"), (i - j) * 8)
                nc.vector.tensor_copy(xd[j][0][:, C:TW], fv[:, 0, ds(i), :].rearrange("p a c -> p (a c)"))
                nc.vector.tensor_copy(xd[j][1][:, C:TW], fv[:, 1, ds(i), :].rearrange("p a c -> p (a c)"))\
                    .then_inc(S("fields_ready"), 1)

            fours(dve, step, 0)

        def dispatch_pool(pool):
            def step(i, j):
                if not (isinstance(i, int) and i < 4):
                    if due((i - j) * 8):
                        pool.wait_ge(S(f"sent{j}"), (i - j) * 8)
                slots_of(pool, i, j)
                pool.wait_ge(S("slots_copied"), i + 1)
                pool.wait_ge(S(f"xd_in{j}"), (i - j) * 8 + 32)
                pool.wait_ge(S("fields_ready"), i + 1)
                pool.sem_inc(S("pool_steps"), 1)
                n = lanes(i)
                for k in range(2):
                    pool.indirect_dma_start(xs_d[:, :], bass.IndirectOffsetOnAxis(ap=idx_d[j][0:n, k:k + 1], axis=0),
                                            xd[j][k][0:n, :], None).then_inc(S(f"sent{j}"), 16)

            fours(pool, step, 0)
            for j in range(4):
                pool.wait_ge(S(f"sent{j}"), 32 * len(range(j, NFULL + 1, 4)))

        def experts_sync(sp):
            def step(i, b):
                if live(i, 0, MT):
                    if due(i - 1):
                        sp.wait_ge(S("fields_taken"), i - 1)
                    sp.dma_start(xs[b][:, :], tile_of(xs_d.rearrange("(t p) c -> t p c", p=P), i)).then_inc(S(f"xs_in{b}"), 16)

            pairs(sp, step, 0, MT)

        def experts_tensor(pe):
            mm = nc.tensor.matmul
            pe.wait_ge(S("w13_in"), 16 * (NE - LATE + NFULL // 4 - 1))
            pe.wait_ge(S("w2_in"), 16 * (NFULL // 4))

            def turn(i, b):
                pe.wait_ge(S(f"xs_in{b}"), after(f"xs_in{b}", (i - b) * 8 + 16))
                if due(i):
                    pe.wait_ge(S("xst_ready"), after("xst_ready", i))
                nc.tensor.transpose(psum[0][:, 0:P], xs[b][:, 0:P], ident[:, :])
                nc.tensor.transpose(psum[0][:, P:C], xs[b][:, P:C], ident[:, :]).then_inc(S("xs_turned"), 1)

            def hidden(i, b, h, e):
                if due(i):
                    pe.wait_ge(S(f"gg{h}_ready"), after(f"gg{h}_ready", i))
                for m in range(2):
                    for c in range(2):
                        last = mm(psum[1 + 2 * h + m][:, 0:FH], xst[b][:, c * P:(c + 1) * P],
                                  w13_sb[:, bass.ds(e * (4 * F) + (c * 2 * F + m * F + h * FH), FH)],
                                  start=(c == 0), stop=(c == 1))
                last.then_inc(S(f"hidden{h}_done"), 1)

            def step(i, b):
                if live(i, 0, MT):
                    if isinstance(i, int) and i == 0:
                        turn(0, 0)
                    e = pe.value_load(et_i[0:1, ds(i)], min_val=0, max_val=NE - 1)
                    pe.wait_ge(S("xst_ready"), after("xst_ready", i + 1))
                    hidden(i, b, 0, e)
                if live(i, 1, MT):
                    if due(i):
                        pe.wait_ge(S("gg1_ready"), after("gg1_ready", i))
                    if due(i - 1):
                        pe.wait_ge(S("ggt_ready"), i - 1)
                    for c in range(4):
                        nc.tensor.transpose(psum[5][:, c * P:(c + 1) * P], gg[1 - b][:, c * P:(c + 1) * P], ident[:, :])
                    nc.tensor.transpose(psum[6][:, 0:P], gg[1 - b][:, 4 * P:5 * P], ident[:, :])
                    nc.tensor.transpose(psum[6][0:FL, P:2 * P], gg[1 - b][:, 5 * P:F], ident[:, :]).then_inc(S("gg_turned"), 1)
                if live(i, 0, MT):
                    hidden(i, b, 1, e)
                    if not isinstance(i, int) or i + 1 < MT:
                        turn(i + 1, 1 - b)
                if live(i, 1, MT):
                    e1 = pe.value_load(et_i[0:1, ds(i - 1)], min_val=0, max_val=NE - 1)
                    if due(i):
                        pe.wait_ge(S("ggt_ready"), i)
                    if due(i - 1):
                        pe.wait_ge(S("yo_ready"), after("yo_ready", i - 1))
                    for c in range(FC):
                        n = P if c < FC - 1 else FL
                        last = mm(psum[7][:, 0:C], ggt[1 - b][0:n, c * P:(c + 1) * P],
                                  w2_sb[0:n, bass.ds(e1 * (FC * C) + c * C, C)], start=(c == 0), stop=(c == FC - 1))
                    last.then_inc(S("y_done"), 1)

            step(0, 0)
            step(1, 1)
            with pe.Fori(1, MT // 2 - 1) as k:
                step(k * 2, 0)
                step(k * 2 + 1, 1)
            for i in range(MT - 2, MT + 1):
                step(i, i % 2)

        def experts_scalar(act):
            a = nc.scalar.activation

            def step(i, b):
                if live(i, 0, MT):
                    if isinstance(i, int) and i == 0:
                        act.wait_ge(S("xs_turned"), after("xs_turned", 1))
                        a(xst[0][:, :], psum[0][:, 0:C], ACT.Copy).then_inc(S("xst_ready"), 1)
                    act.wait_ge(S("hidden0_done"), after("hidden0_done", i + 1))
                    if due(i):
                        act.wait_ge(S("gg0_ready"), after("gg0_ready", i))
                    a(sig[0][:, :], psum[1][:, 0:FH], ACT.Sigmoid).then_inc(S("sig0_ready"), 1)
                if live(i, 1, MT):
                    if due(i):
                        act.wait_ge(S("gg_turned"), after("gg_turned", i))
                    if due(i - 2):
                        act.wait_ge(S("y_done"), after("y_done", i - 2))
                    a(ggt[1 - b][:, 0:4 * P], psum[5][:, :], ACT.Copy)
                    a(ggt[1 - b][:, 4 * P:5 * P], psum[6][:, 0:P], ACT.Copy)
                    a(ggt[1 - b][0:FL, 5 * P:6 * P], psum[6][0:FL, P:2 * P], ACT.Copy).then_inc(S("ggt_ready"), 1)
                if live(i, 0, MT):
                    act.wait_ge(S("hidden1_done"), after("hidden1_done", i + 1))
                    if due(i):
                        act.wait_ge(S("gg1_ready"), after("gg1_ready", i))
                    a(sig[1][:, :], psum[3][:, 0:FH], ACT.Sigmoid).then_inc(S("sig1_ready"), 1)
                    if not isinstance(i, int) or i + 1 < MT:
                        act.wait_ge(S("xs_turned"), after("xs_turned", i + 2))
                        if due(i):
                            act.wait_ge(S("hidden1_done"), after("hidden1_done", i))
                        a(xst[1 - b][:, :], psum[0][:, 0:C], ACT.Copy).then_inc(S("xst_ready"), 1)
                if live(i, 1, MT):
                    if due(i):
                        act.wait_ge(S("y_done"), after("y_done", i))
                    if not (isinstance(i, int) and i - 1 < 2):
                        if due((i - 1 - (1 - b)) * 8):
                            act.wait_ge(S(f"added{1 - b}"), after(f"added{1 - b}", (i - 1 - (1 - b)) * 8))
                    act.wait_ge(S("fields_taken"), i)
                    a(yo[1 - b][:, :], psum[7][:, 0:C], ACT.Copy, scale=slot_gate[1 - b][:, :]).then_inc(S("yo_ready"), 1)

            step(0, 0)
            step(1, 1)
            with act.Fori(1, MT // 2 - 1) as k:
                step(k * 2, 0)
                step(k * 2 + 1, 1)
            for i in range(MT - 2, MT + 1):
                step(i, i % 2)

        def experts_vector(dve):
            v = nc.vector

            def step(i, b):
                for h in range(2):
                    dve.wait_ge(S(f"sig{h}_ready"), after(f"sig{h}_ready", i + 1))
                    if due(i):
                        dve.wait_ge(S(f"gg{h}_ready"), after(f"gg{h}_ready", i))
                    v.tensor_tensor(prod1[h][:, :], psum[1 + 2 * h][:, 0:FH], sig[h][:, :], ALU.mult).then_inc(S(f"silu{h}"), 1)
                    dve.wait_ge(S(f"silu{h}"), i + 1)
                    if due(i - 1):
                        dve.wait_ge(S("gg_turned"), after("gg_turned", i - 1))
                    v.tensor_tensor(gg[b][:, h * FH:(h + 1) * FH], psum[2 + 2 * h][:, 0:FH], prod1[h][:, :], ALU.mult)\
                        .then_inc(S(f"gg{h}_ready"), 1)
                dve.wait_ge(S(f"xs_in{b}"), after(f"xs_in{b}", (i - b) * 8 + 16))
                if due(i):
                    dve.wait_ge(S("fields_taken"), i)
                v.tensor_scalar(unused[:, :], xs[b][:, C:C + 1], 0.0, spare[:, :], ALU.is_equal, ALU.mult)\
                    .then_inc(S("unused_ready"), 1)
                dve.wait_ge(S("unused_ready"), i + 1)
                if not (isinstance(i, int) and i < 2):
                    dve.wait_ge(S("yo_ready"), after("yo_ready", i - 1))
                    dve.wait_ge(S(f"added{b}"), after(f"added{b}", (i - b) * 8))
                v.tensor_copy(slot_gate[b][:, :], xs[b][:, C + 1:C + 2])
                v.scalar_tensor_tensor(slot_row[b][:, :], unused[:, :], -1.0, xs[b][:, C:C + 1], ALU.add, ALU.add)\
                    .then_inc(S("fields_taken"), 1)

            pairs(dve, step, 0, MT)

        def experts_pool(pool):
            def step(i, b):
                pool.wait_ge(S("fields_taken"), i + 1)
                pool.wait_ge(S("yo_ready"), after("yo_ready", i + 1))
                if due(i):
                    pool.wait_ge(S(f"added{1 - b}"), after(f"added{1 - b}", (i + b) * 8))
                pool.sem_inc(S("pool_steps"), 1)
                pool.indirect_dma_start(out[:, :], bass.IndirectOffsetOnAxis(ap=slot_row[b][:, 0:1], axis=0), yo[b][:, :], None,
                                        compute_op=ALU.add).then_inc(S(f"added{b}"), 16)

            pairs(pool, step, 0, MT)
            for b in range(2):
                pool.wait_ge(S(f"added{b}"), after(f"added{b}", 8 * MT))

        def sort_pool(pool):
            pool.iota(iota_i[:, :], pattern=[[1, P]], base=0, channel_multiplier=0).then_inc(S("iota_ready"), 1)
            pool.iota(tile_i[:, :], pattern=[[1, GT]], base=0, channel_multiplier=0)
            pool.iota(lane_i[:, :], pattern=[[P, NT]], base=0, channel_multiplier=1).then_inc(S("pool_lanes"), 1)
            pool.iota(token_i[:, :], pattern=[[P, NT]], base=1, channel_multiplier=1)
            pool.iota(spare_i[:, :], pattern=[[P, 1]], base=NT * P + 1, channel_multiplier=1)
            pool.memset(ident[:, :], 0.0)
            pool.memset(before[:, :], 1.0).then_inc(S("pool_set"), 1)
            pool.wait_ge(S("pool_set"), 1)
            pool.affine_select(out=ident[:, :], in_=ident[:, :], compare_op=ALU.not_equal, fill=1.0, base=0,
                               pattern=[[-1, P]], channel_multiplier=1)
            pool.affine_select(out=before[:, :], in_=before[:, :], compare_op=ALU.is_gt, fill=0.0, base=0,
                               pattern=[[1, P]], channel_multiplier=-1).then_inc(S("consts_ready"), 1)
            pool.wait_ge(S("rec_cleared"), 16)

            def chunk(k, b):
                pool.wait_ge(S("slots_ready"), k + 1)
                if not (isinstance(k, int) and k < 2):
                    if due((k - b) * (8 * EC)):
                        pool.wait_ge(S(f"sort_scattered{b}"), (k - b) * (8 * EC))
                pool.tensor_copy(idx_ring[:, b * EC:(b + 1) * EC], slot_i[:, bass.ds(k * EC, EC)])
                pool.tensor_copy(rec_ring[:, b * 2 * EC:(b + 1) * 2 * EC],
                                 rec[:, bass.ds(k * (2 * EC), 2 * EC)]).then_inc(S("ring_filled"), 1)
                pool.wait_ge(S("ring_filled"), k + 1)
                pool.sem_inc(S("pool_steps"), 1)
                for j in range(EC):
                    r = b * EC + j
                    pool.indirect_dma_start(rec_d[:, :], bass.IndirectOffsetOnAxis(ap=idx_ring[:, r:r + 1], axis=0),
                                            rec_ring[:, 2 * r:2 * r + 2], None).then_inc(S(f"sort_scattered{b}"), 16)

            chunk(0, 0)
            chunk(1, 1)
            with pool.Fori(1, NCH // 2) as i:
                chunk(i * 2, 0)
                chunk(i * 2 + 1, 1)

        def sort_vector(dve):
            v = nc.vector
            o = Order(dve, "v_sort")
            v.memset(row_i[:, FULL:ET], 49 * P)
            v.memset(col_i[:, FULL:ET], DUMMY).then_inc(S("edges_cleared"), 1)
            ri = rec_init.rearrange("p (t c) -> p t c", c=2)
            v.memset(ri[:, :, 0], -1).then_inc(S("rec_init_ready"), 1)
            v.memset(ri[:, :, 1], DUMMY).then_inc(S("rec_init_ready"), 1)
            v.memset(ones[:, :], 1.0).then_inc(S("ones_ready"), 1)
            v.memset(zeros[:, :], 0.0).then_inc(S("zeros_ready"), 1)
            o(v.memset(scan[:, :], 0.0))
            dve.wait_ge(S("iota_ready"), 1)
            o(v.tensor_copy(iota[:, :], iota_i[:, :]))
            dve.wait_ge(S("edges_in"), 64)
            rc = rec.rearrange("p (t c) -> p t c", c=2)
            o(v.tensor_scalar(hi_i[:, :], row_i[:, :], 7, None, ALU.logical_shift_right))
            v.tensor_scalar(rc[:, :, 0], row_i[:, :], P - 1, None, ALU.bitwise_and)
            v.tensor_copy(rc[:, :, 1], col_i[:, :])
            dve.wait_ge(S("v_sort"), o.n)
            o(v.tensor_copy(hi_f[:, :], hi_i[:, :]))
            o(v.tensor_copy(hi_b[:, :], hi_i[:, :]))
            dve.wait_ge(S("v_sort"), o.n)
            def count(i):
                v.tensor_scalar(mask[0][:, :], hi_b[:, :], iota[:, ds(i * 2)], None, ALU.is_equal).then_inc(S("hist_mask"), 1)
                if due(i):
                    dve.wait_ge(S("hist_acted"), i)
                v.tensor_scalar(mask[1][:, :], hi_b[:, :], iota[:, ds(i * 2 + 1)], None, ALU.is_equal).then_inc(S("hist_mask"), 1)
                dve.wait_ge(S("hist_mask"), i * 2 + 1)
                v.tensor_reduce(hist[:, ds(i * 2)], mask[0][:, :], AX.X, ALU.add).then_inc(S("hist_done"), 1)
                dve.wait_ge(S("hist_done"), i + 1)
                dve.sem_inc(S("vector_steps"), 1)

            count(0)
            with dve.Fori(1, NT // 2) as i:
                count(i)
            dve.wait_ge(S("hist_sums"), 1)
            o(v.tensor_scalar(tiles_i[:, :], psum[0][:, 0:NT], float(P - 1), None, ALU.add))
            dve.wait_ge(S("v_sort"), o.n)
            o(v.tensor_scalar(tiles_i[:, :], tiles_i[:, :], 7, None, ALU.logical_shift_right))
            dve.wait_ge(S("v_sort"), o.n)
            W = 64 + NT
            o(v.tensor_copy(scan[:, 64:W], tiles_i[:, :]))
            dve.wait_ge(S("v_sort"), o.n)
            cur = 0
            for d in (1, 2, 4, 8, 16, 32):
                a, b = cur * W, (1 - cur) * W
                o(v.tensor_tensor(scan[:, b + 64:b + W], scan[:, a + 64:a + W], scan[:, a + 64 - d:a + W - d], ALU.add))
                dve.wait_ge(S("v_sort"), o.n)
                cur = 1 - cur
            o(v.tensor_copy(first[:, NT:2 * NT], scan[:, cur * W + 64:cur * W + W]))
            o(v.tensor_tensor(first[:, 0:NT], scan[:, cur * W + 64:cur * W + W], tiles_i[:, :], ALU.subtract))
            dve.wait_ge(S("v_sort"), o.n)
            v.scalar_tensor_tensor(run[:, 0:NT], first[:, 0:NT], float(P), psum[0][:, 64:64 + NT], ALU.mult, ALU.add)\
                .then_inc(S("first_ready"), 1)
            dve.wait_ge(S("first_ready"), 1)
            oh = onehot.rearrange("p (t b) -> p t b", b=NT)
            with dve.Fori(0, NCH) as k:
                v.tensor_tensor(oh, hi_f[:, bass.ds(k * EC, EC)].unsqueeze(2).to_broadcast([P, EC, NT]),
                                iota[:, 0:NT].unsqueeze(1).to_broadcast([P, EC, NT]), ALU.is_equal).then_inc(S("chain"), 1)
                c = 1
                for j in range(EC):
                    a, b = (j % 2) * NT, (1 - j % 2) * NT
                    dve.wait_ge(S("chain"), k * (EC + 4) + c)
                    v.tensor_tensor_reduce(junk[:, :], oh[:, j, :], run[:, a:a + NT], 1.0, 0.0, ALU.mult, ALU.add,
                                           chunk_pos[:, j:j + 1])
                    v.tensor_tensor(run[:, b:b + NT], run[:, a:a + NT], oh[:, j, :], ALU.add).then_inc(S("chain"), 1)
                    c += 1
                dve.wait_ge(S("chain"), k * (EC + 4) + c)
                v.tensor_copy(chunk_i[:, 0:EC], chunk_pos[:, :]).then_inc(S("chain"), 1)
                dve.wait_ge(S("chain"), k * (EC + 4) + c + 1)
                v.tensor_scalar(chunk_i[:, EC:2 * EC], chunk_i[:, 0:EC], 7, None, ALU.logical_shift_right)
                v.tensor_scalar(chunk_i[:, 0:EC], chunk_i[:, 0:EC], P - 1, None, ALU.bitwise_and).then_inc(S("chain"), 1)
                dve.wait_ge(S("chain"), k * (EC + 4) + c + 2)
                v.scalar_tensor_tensor(slot_i[:, bass.ds(k * EC, EC)], chunk_i[:, 0:EC], float(GT), chunk_i[:, EC:2 * EC],
                                       ALU.mult, ALU.add).then_inc(S("slots_ready"), 1)
                dve.wait_ge(S("slots_ready"), k + 1)
                dve.sem_inc(S("chain"), 1)


        @block.sync
        def _(sp):
            sort_sync(sp)
            project_sync(sp)
            sp.wait_ge(S("sort_scattered0"), 16 * EC * (NCH // 2))
            sp.wait_ge(S("sort_scattered1"), 16 * EC * (NCH // 2))
            phase(sp, 1)
            sp.dma_start(rec_all[:, :], rec_d.rearrange("(p t) c -> p (t c)", p=P)).then_inc(S("records_in"), 16)
            phase(sp, 2)
            route_sync(sp)
            phase(sp, 3)
            dispatch_sync(sp)
            phase(sp, 4)
            experts_sync(sp)

        @block.gpsimd
        def _(pool):
            sort_pool(pool)
            phase(pool, 1)
            gather_pool(pool)
            phase(pool, 2)
            phase(pool, 3)
            dispatch_pool(pool)
            phase(pool, 4)
            experts_pool(pool)

        @block.vector
        def _(dve):
            sort_vector(dve)
            project_vector(dve)
            mix_vector(dve)
            tables_vector(dve)
            phase(dve, 1)
            gather_vector(dve)
            phase(dve, 2)
            route_vector(dve)
            phase(dve, 3)
            dispatch_vector(dve)
            phase(dve, 4)
            experts_vector(dve)

        @block.tensor
        def _(pe):
            pe.wait_ge(S("consts_ready"), 1)
            pe.wait_ge(S("ones_ready"), 1)
            pe.wait_ge(S("hist_done"), NT // 2)
            pe.wait_ge(S("hist_acted"), NT // 2)
            nc.tensor.matmul(psum[0][:, 0:NT], ones[:, :], hist[:, :], start=True, stop=True)
            nc.tensor.matmul(psum[0][:, 64:64 + NT], before[:, :], hist[:, :], start=True, stop=True).then_inc(S("hist_sums"), 1)
            pe.wait_ge(S("first_ready"), 1)
            project_tensor(pe)
            mix_tensor(pe)
            tables_tensor(pe)
            phase(pe, 1)
            gather_tensor(pe)
            phase(pe, 2)
            route_tensor(pe)
            phase(pe, 3)
            phase(pe, 4)
            experts_tensor(pe)

        @block.scalar
        def _(act):
            sort_scalar(act)
            project_scalar(act)
            mix_scalar(act)
            phase(act, 1)
            gather_scalar(act)
            phase(act, 2)
            route_scalar(act)
            phase(act, 3)
            phase(act, 4)
            experts_scalar(act)

def kernel(**inputs):
    import numpy as _np
    import concourse.bacc as _bacc
    from concourse import mybir as _mybir
    from concourse.bass_utils import run_bass_kernel_spmd as _run

    g = {k: _np.ascontiguousarray(v) for k, v in inputs.items()}
    pad = _np.zeros((NT * P, C), _np.float32)
    pad[0:N] = g["x"]
    w1, w3, w2 = g["L0_ffn_w1"], g["L0_ffn_w3"], g["L0_ffn_w2"]
    w13 = _np.concatenate([w1.transpose(2, 0, 1), w3.transpose(2, 0, 1)], 2)
    w13 = w13.reshape(2, P, NE, 2 * F).transpose(1, 2, 0, 3)
    w2p = _np.zeros((NE, FC * P, C), _np.float32)
    w2p[:, 0:F] = w2.transpose(0, 2, 1)
    w2p = w2p.reshape(NE, FC, P, C).transpose(2, 0, 1, 3)
    qkv = g["L0_mix_W_qkv"]
    named = {
        "x": pad, "src": g["src"], "dst": g["dst"],
        "w_h": g["L0_gnn_W_layer"], "w_hT": g["L0_gnn_W_layer"].T, "b_h": g["L0_gnn_b_layer"],
        "w_a": _np.concatenate([g["L0_gnn_w_a1"], g["L0_gnn_w_a2"]], 0).T,
        "b_a": _np.concatenate([g["L0_gnn_b_a1"], g["L0_gnn_b_a2"]], 0),
        "w_qkv": qkv, "w_vT": qkv[:, 2 * C:].T, "b_qkv": g["L0_mix_b_qkv"],
        "w_out": g["L0_mix_W_out"], "b_out": g["L0_mix_b_out"],
        "b_cols": _np.stack([g["L0_mix_b_qkv"][2 * C:2 * C + P], g["L0_mix_b_qkv"][2 * C + P:], g["L0_gnn_b_layer"][:P],
                             g["L0_gnn_b_layer"][P:]], 1),
        "w_router": g["L0_ffn_router_w"].T, "w13": w13.reshape(P, -1), "w2": w2p.reshape(P, -1),
    }
    nc = _bacc.Bacc("TRN2", target_bir_lowering=False, num_devices=1)
    arrays, args = {}, []
    for name, a in named.items():
        arrays[f"in_{name}"] = _np.ascontiguousarray(a)
        args.append(nc.dram_tensor(f"in_{name}", a.shape, _mybir.dt.from_np(a.dtype), kind="ExternalInput").ap())
    args.append(nc.dram_tensor("out", (NT * P + P, C), F32, kind="ExternalOutput").ap())
    build(nc, *args)
    r = _run(nc, [arrays], core_ids=[0])
    return r.results[0]["out"][0:N]
```
